# Optimizing a Trainium2 kernel written in Bass

```python
import numpy as np
import jax
import jax.numpy as jnp

def _softmax(x, axis=-1):
    return jax.nn.softmax(x, axis=axis)

def _gelu(x):
    return jax.nn.gelu(x, approximate=True)

def _silu(x):
    return jax.nn.silu(x)

def _sigmoid(x):
    return jax.nn.sigmoid(x)

def _layernorm(x, axis=-1, eps=1e-05):
    m = jnp.mean(x, axis=axis, keepdims=True)
    v = jnp.var(x, axis=axis, keepdims=True)
    return (x - m) / jnp.sqrt(v + eps)

def _scatter_add(tgt, idx, src, axis=0):
    return tgt.at[idx].add(src)

def _segment_sum(src, seg, n):
    return jax.ops.segment_sum(src, seg, n)
kernel_name = 'mk_sandwich_d1_jaxref_r8_334992'

def setup_inputs(seed: int=0):
    np.random.seed(seed)
    _w = jnp.asarray

    def _L0_attn_setup():
        import jax, jax.numpy as jnp
        import numpy as np
        B, S, HID = (2, 256, 512)
        NH, NKV = (32, 8)
        HD = HID // NH
        G = NH // NKV
        ROPE_THETA = 10000.0

        def _rope_cos_sin(seq_len, head_dim, dtype):
            inv_freq = 1.0 / ROPE_THETA ** (jnp.arange(0, head_dim, 2, dtype=jnp.float32) / head_dim)
            pos = jnp.arange(seq_len, dtype=jnp.float32)
            freqs = pos[:, None] * inv_freq[None, :]
            emb = jnp.concatenate([freqs, freqs], axis=-1)
            return (jnp.cos(emb).astype(dtype), jnp.sin(emb).astype(dtype))

        def _rotate_half(x):
            x1, x2 = jnp.split(x, 2, axis=-1)
            return jnp.concatenate([-x2, x1], axis=-1)

        def _apply_rope(x, cos, sin):
            return x * cos[None, None] + _rotate_half(x) * sin[None, None]
        key = jax.random.key(seed)
        ks = jax.random.split(key, 5)
        scale = 0.02
        return {'hidden_states': jax.random.normal(ks[0], (B, S, HID), dtype=jnp.float32), 'Wq': jax.random.normal(ks[1], (NH * HD, HID), dtype=jnp.float32) * scale, 'Wk': jax.random.normal(ks[2], (NKV * HD, HID), dtype=jnp.float32) * scale, 'Wv': jax.random.normal(ks[3], (NKV * HD, HID), dtype=jnp.float32) * scale, 'Wo': jax.random.normal(ks[4], (HID, HID), dtype=jnp.float32) * scale}
    _L0_attn_in = _L0_attn_setup()

    def _L0_ffn_setup():
        import jax, jax.numpy as jnp
        import numpy as np
        HIDDEN = 512
        INTER = 1376

        def _ternary_quantize(w):
            scale = jnp.mean(jnp.abs(w))
            return jnp.clip(jnp.round(w / scale), -1.0, 1.0) * scale
        key = jax.random.key(seed)
        kx, kg, ku, kd = jax.random.split(key, 4)
        x = jax.random.normal(kx, (2, 256, HIDDEN), dtype=jnp.float32)
        w_gate = _ternary_quantize(jax.random.normal(kg, (INTER, HIDDEN), dtype=jnp.float32) * 0.02)
        w_up = _ternary_quantize(jax.random.normal(ku, (INTER, HIDDEN), dtype=jnp.float32) * 0.02)
        w_down = _ternary_quantize(jax.random.normal(kd, (HIDDEN, INTER), dtype=jnp.float32) * 0.02)
        return {'x': x, 'w_gate': w_gate, 'w_up': w_up, 'w_down': w_down}
    _L0_ffn_in = _L0_ffn_setup()
    _d = {'L0_attn_hidden_states': _L0_attn_in['hidden_states'], 'L0_attn_Wq': _L0_attn_in['Wq'], 'L0_attn_Wk': _L0_attn_in['Wk'], 'L0_attn_Wv': _L0_attn_in['Wv'], 'L0_attn_Wo': _L0_attn_in['Wo'], 'L0_ffn_w_gate': _L0_ffn_in['w_gate'], 'L0_ffn_w_up': _L0_ffn_in['w_up'], 'L0_ffn_w_down': _L0_ffn_in['w_down']}
    _x0 = _d['L0_attn_hidden_states']
    _d['L0_attn_hidden_states'] = jax.random.normal(jax.random.fold_in(jax.random.key(seed), 1), (2, 512, 512), dtype=_x0.dtype)
    del _x0
    return _d

def reference(L0_attn_hidden_states, L0_attn_Wq, L0_attn_Wk, L0_attn_Wv, L0_attn_Wo, L0_ffn_w_gate, L0_ffn_w_up, L0_ffn_w_down):

    def _L0_attn_ref(hidden_states, Wq, Wk, Wv, Wo):
        import jax, jax.numpy as jnp
        import numpy as np
        B, S, HID = (2, 256, 512)
        NH, NKV = (32, 8)
        HD = HID // NH
        G = NH // NKV
        ROPE_THETA = 10000.0

        def _rope_cos_sin(seq_len, head_dim, dtype):
            inv_freq = 1.0 / ROPE_THETA ** (jnp.arange(0, head_dim, 2, dtype=jnp.float32) / head_dim)
            pos = jnp.arange(seq_len, dtype=jnp.float32)
            freqs = pos[:, None] * inv_freq[None, :]
            emb = jnp.concatenate([freqs, freqs], axis=-1)
            return (jnp.cos(emb).astype(dtype), jnp.sin(emb).astype(dtype))

        def _rotate_half(x):
            x1, x2 = jnp.split(x, 2, axis=-1)
            return jnp.concatenate([-x2, x1], axis=-1)

        def _apply_rope(x, cos, sin):
            return x * cos[None, None] + _rotate_half(x) * sin[None, None]
        bsz, q_len, _ = hidden_states.shape
        dt = hidden_states.dtype
        q = (hidden_states @ Wq.T).reshape(bsz, q_len, NH, HD).transpose(0, 2, 1, 3)
        k = (hidden_states @ Wk.T).reshape(bsz, q_len, NKV, HD).transpose(0, 2, 1, 3)
        v = (hidden_states @ Wv.T).reshape(bsz, q_len, NKV, HD).transpose(0, 2, 1, 3)
        cos, sin = _rope_cos_sin(q_len, HD, dt)
        q = _apply_rope(q, cos, sin)
        k = _apply_rope(k, cos, sin)
        qg = q.reshape(bsz, NKV, G, q_len, HD)
        scores = jnp.einsum('bkgqd,bkvd->bkgqv', qg, k) * (1.0 / np.sqrt(HD))
        causal = jnp.tril(jnp.ones((q_len, q_len), dtype=bool))
        scores = jnp.where(causal[None, None, None], scores, jnp.finfo(jnp.float32).min)
        probs = jax.nn.softmax(scores.astype(jnp.float32), axis=-1).astype(dt)
        out = jnp.einsum('bkgqv,bkvd->bkgqd', probs, v)
        out = out.reshape(bsz, NH, q_len, HD).transpose(0, 2, 1, 3).reshape(bsz, q_len, HID)
        return out @ Wo.T

    def _L0_ffn_ref(x, w_gate, w_up, w_down):
        import jax, jax.numpy as jnp
        import numpy as np
        HIDDEN = 512
        INTER = 1376

        def _ternary_quantize(w):
            scale = jnp.mean(jnp.abs(w))
            return jnp.clip(jnp.round(w / scale), -1.0, 1.0) * scale
        xf = x.astype(jnp.float32) / 128.0
        gate = jnp.einsum('bsh,ih->bsi', xf, w_gate)
        up = jnp.einsum('bsh,ih->bsi', xf, w_up)
        inter = jax.nn.silu(gate) * up
        inter_q = jnp.trunc(jnp.clip(inter * 128.0, -128.0, 127.0)).astype(jnp.int8)
        down = jnp.einsum('bsi,hi->bsh', inter_q.astype(jnp.float32), w_down)
        out = jnp.trunc(jnp.clip(down * 128.0, -128.0, 127.0)).astype(jnp.int8)
        return out
    x = L0_attn_hidden_states
    x = x + _layernorm(_L0_attn_ref(_layernorm(x, axis=-1), L0_attn_Wq, L0_attn_Wk, L0_attn_Wv, L0_attn_Wo), axis=-1)
    x = x + _layernorm(_L0_ffn_ref(_layernorm(x, axis=-1), L0_ffn_w_gate, L0_ffn_w_up, L0_ffn_w_down), axis=-1)
    return x

_drawn_inputs = setup_inputs


def setup_inputs(seed=0):
    import zlib

    import numpy as np

    out = dict(_drawn_inputs(seed))
    spreads = {}
    factors = {}
    for name, (base, spread) in spreads.items():
        noise = np.random.default_rng([zlib.crc32(name.encode()), seed]).standard_normal(out[name].shape)
        drawn = base * np.exp(spread * noise) if base else spread * noise
        out[name] = jnp.asarray(drawn.astype(out[name].dtype))
    for name, factor in factors.items():
        out[name] = (out[name] * factor).astype(out[name].dtype)
    return out
```

```python
from contextlib import ExitStack

import numpy as np

import concourse.bass as bass
from concourse import mybir

F32 = mybir.dt.float32
F32R = mybir.dt.float32r
BF16 = mybir.dt.bfloat16
ALU = mybir.AluOpType
ACT = mybir.ActivationFunctionType
AX = mybir.AxisListType

P = 128
B, S, D = 2, 512, 512
TOK = B * S
NT = TOK // P
TB = S // P
KD = D // P
NH, NKV, HD = 32, 8, 16
G = NH // NKV
NPAIR = G // 2
SLOT = 64
MROW = 3 * HD
QKVW = D + 2 * NKV * HD
NQK = (D + NKV * HD) // P
NPROJ = QKVW // P
F = 1376
NF = -(-F // P)
EPS = 1e-5
IN_SCALE = 128.0
OUT_SCALE = 128.0
NEG = -1.0e38
MAGIC = 8388608.0
SCALE = 1.0 / np.sqrt(HD)
ITERS = B * NKV

MAX_STEPS = [(0, (0, 1, 2, 3), P)] + [(1, (0, 1), 2 * P), (1, (2, 3), 2 * P)] \
    + [(i, (h,), (i + 1) * P) for i in (2, 3) for h in range(G)]
SCORE_STEPS = [(0, (0,)), (0, (1,)), (1, (0,)), (1, (1,)), (2, (0, 1)), (3, (0, 1))]
NM, NS = len(MAX_STEPS), len(SCORE_STEPS)
BODY = ["OT", "S0", "M0", "MT", "M1", "S1", "M2", "B0", "M3", "S2", "PV0", "M4", "S3", "B1",
        "M5", "S4", "PV1", "M6", "S5", "B2", "M7", "PV2", "M8", "PV3", "M9", "M10"]
LAG = {"B": 0, "M": 1, "MT": 2, "S": 3, "PV": 3, "OT": 4}
MISC = ("OT", "MT", "B0", "B1", "B2")
NB = 4


def kind_of(step):
    return step if step in ("MT", "OT") else step.rstrip("0123456789")


def body_steps():
    for j in range(ITERS + max(LAG.values())):
        for step in BODY:
            n = j - LAG[kind_of(step)]
            if 0 <= n < ITERS:
                yield j, step, n


def misc_counts():
    before, after, done = {}, {}, 0
    for _, step, n in body_steps():
        if step in MISC:
            before[step, n] = done
            done += 2 if step == "B2" else 1
            after[step, n] = done
    return before, after


def layer_kernel(nc, x_in, wqkvT, woT, wguT, wdT, cosT, sinT, eye, out):
    with ExitStack() as ctx:
        at = [16512]

        def place(name, shape, dt, offset=None):
            size = 4 if dt in (F32, F32R) else 2
            nbytes = int(np.prod(shape[1:])) * size
            if offset is None:
                offset = at[0]
                at[0] += -(-nbytes // 32) * 32
            return nc.alloc_sbuf_tensor_at(name, shape, dt, offset=offset), offset + nbytes

        def sem(name):
            return ctx.enter_context(nc.semaphore(name))

        x, _ = place("x", [P, NT, D], F32)
        a_xt = at[0]
        xTh, _ = place("xTh", [P, KD, TOK], F32R)
        xTl, _ = place("xTl", [P, KD, TOK], F32R)
        woh, _ = place("woh", [P, KD, D], F32R)
        wol, _ = place("wol", [P, KD, D], F32R)
        a_o = at[0]
        o_nat, _ = place("o_nat", [P, NT, D], F32)
        a_g = at[0]
        qkh0, e = place("qkh0", [P, NQK, S], F32R)
        qkl0, e = place("qkl0", [P, NQK, S], F32R)
        a_r2 = at[0]
        qkh1, e = place("qkh1", [P, NQK, S], F32R)
        qkl1, e = place("qkl1", [P, NQK, S], F32R)
        vone, e = place("vone", [P, NT, NKV, 32], F32)
        a_cos = at[0]
        cos_sb, e = place("cos_sb", [P, S], F32)
        sin_sb, e = place("sin_sb", [P, S], F32)
        selqh, e = place("selqh", [P, 8, 4, HD], F32R)
        selql, e = place("selql", [P, 8, 4, HD], F32R)
        selkh, e = place("selkh", [P, NKV, 2, 4, HD], F32R)
        selkl, e = place("selkl", [P, NKV, 2, 4, HD], F32R)
        a_r1 = at[0]
        qst = [place(f"qst{i}", [P, NPAIR, S], F32R)[0] for i in range(NB)]
        kst = [place(f"kst{i}", [P, 2, S], F32R)[0] for i in range(NB)]
        probs, e = place("probs", [P, NS, 2 * S], F32)
        ots = [place(f"ots{i}", [P, S], F32)[0] for i in range(2)]
        a_r1_end = at[0]
        identf, _ = place("identf", [P, P], F32)
        identb, _ = place("identb", [P, P], BF16)
        maskb, _ = place("maskb", [P, P], BF16)
        zerob, _ = place("zerob", [P, P], BF16)
        ones_row, _ = place("ones_row", [P, 1], F32)
        epsc, _ = place("epsc", [P, 1], F32)
        mx = [place(f"mx{i}", [P, TB, G], F32)[0] for i in range(2)]
        ms = [place(f"ms{i}", [P, TB, G, 2], F32R)[0] for i in range(2)]
        rden = [place(f"rden{i}", [P, TB, G], F32)[0] for i in range(2)]
        stats, _ = place("stats", [P, NT, 6], F32)
        mv, _ = place("mv", [P, 4, NT, 2], F32)
        sd, _ = place("sd", [P, 4, NT], F32)
        rstd, _ = place("rstd", [P, 4, NT], F32)
        assert at[0] <= 229368, at[0]

        wq_raw, e = place("wq_raw", [P, KD, QKVW], F32, a_r1)
        wqh, e = place("wqh", [P, KD, QKVW], F32R, e)
        wql, e = place("wql", [P, KD, QKVW], F32R, e)
        xn = [None, None]
        xn[0], e = place("xn0", [P, D], F32, e)
        xn[1], e = place("xn1", [P, D], F32, e)
        rope_u, rope_s, rope_v, rope_r = [None] * 2, [None] * 2, [None] * 2, [None] * 2
        for i in range(2):
            rope_u[i], e = place(f"rope_u{i}", [P, S], F32, e)
            rope_s[i], e = place(f"rope_s{i}", [P, S], F32, e)
            rope_v[i], e = place(f"rope_v{i}", [P, S], F32, e)
        assert e <= a_r1_end, (e, a_r1_end)
        for i in range(2):
            rope_r[i], e = place(f"rope_r{i}", [P, S], F32, a_o + 2048 * i)
        vT = [place(f"vT{i}", [P, S], F32, a_o + 4096 + 2048 * i)[0] for i in range(2)]
        mt = [place(f"mt{i}", [2 * G, S], F32R, a_cos + 2048 * i)[0] for i in range(2)]
        wo_raw, _ = place("wo_raw", [P, KD, D], F32, a_xt)
        interq, e1 = place("interq", [P, NF, TOK], F32R, a_r1)
        oth, otl = [None] * 2, [None] * 2
        e = a_r1
        for i in range(2):
            oth[i], e = place(f"oth{i}", [P, KD, P], F32R, e)
            otl[i], e = place(f"otl{i}", [P, KD, P], F32R, e)
        tmp, e1 = place("tmp", [P, D], F32, e1)
        xn2 = [None] * 2
        xn2[0], e1 = place("xn2_0", [P, D], F32, e1)
        xn2[1], e1 = place("xn2_1", [P, D], F32, e1)
        wd_raw = [None] * 2
        wd_raw[0], e1 = place("wd_raw0", [P, D], F32, e1)
        assert e1 <= a_r1_end, (e1, a_r1_end)
        wdh, e = place("wdh", [P, NF, D], F32R, a_r2)
        wdl, e = place("wdl", [P, NF, D], F32R, e)
        assert e <= a_r1
        guh, gul = [None] * 2, [None] * 2
        e = a_g
        for i in range(2):
            guh[i], e = place(f"guh{i}", [P, KD, 2, P], F32R, e)
            gul[i], e = place(f"gul{i}", [P, KD, 2, P], F32R, e)
        gu_raw, e = place("gu_raw", [P, KD, 2, P], F32, e)
        assert e <= a_r2
        f_names = ("silu", "clip", "absv", "sign", "rnd", "above", "flo", "y")
        ft = {}
        e = a_o
        for k in f_names:
            ft[k], e = place("f_" + k, [P, S], F32, e)
        e = a_xt + 2 * 16384
        ft2 = {}
        for k in f_names:
            ft2[k], e = place("g_" + k, [P, S], F32, e)
        ftmp = [ft, ft2]

        ps = ctx.enter_context(nc.psum_tensor("ps", [P, 8, 512], F32))

        x_loaded = [sem(f"x_loaded{t}") for t in range(NT)]
        wq_loaded = [sem(f"wq_loaded{k}") for k in range(KD)]
        tab_loaded = sem("tab_loaded")
        wo_loaded = sem("wo_loaded")
        gu_loaded = sem("gu_loaded")
        wd_loaded = sem("wd_loaded")
        out_stored = sem("out_stored")
        consts_ready = sem("consts_ready")
        kzero_ready = sem("kzero_ready")
        sel_ready = sem("sel_ready")
        wq_hi, wq_lo = sem("wq_hi"), sem("wq_lo")
        wo_hi, wo_lo = sem("wo_hi"), sem("wo_lo")
        gu_hi, gu_lo = sem("gu_hi"), sem("gu_lo")
        wd_hi, wd_lo = sem("wd_hi"), sem("wd_lo")
        dve_step = sem("dve_step")
        var_ready = sem("var_ready")
        sd_ready = sem("sd_ready")
        xn_ready = sem("xn_ready")
        xt_psum = sem("xt_psum")
        xt_hi, xt_lo = sem("xt_hi"), sem("xt_lo")
        proj_done = sem("proj_done")
        shuf_done = sem("shuf_done")
        rope_prod = sem("rope_prod")
        rope_sum = sem("rope_sum")
        qk_hi, qk_lo = sem("qk_hi"), sem("qk_lo")
        vt_copied = sem("vt_copied")
        v_psum = sem("v_psum")
        v_ready = sem("v_ready")
        stack_psum = sem("stack_psum")
        misc_read = sem("misc_read")
        max_psum = sem("max_psum")
        max_red = sem("max_red")
        max_split = sem("max_split")
        mt_psum = sem("mt_psum")
        mrow_sent = [sem(f"mrow_sent{i}") for i in range(NB)]
        score_psum = sem("score_psum")
        exp_done = sem("exp_done")
        masked = sem("masked")
        pv_done = sem("pv_done")
        ot_copied = sem("ot_copied")
        ot_psum = sem("ot_psum")
        rden_ready = sem("rden_ready")
        or_psum = sem("or_psum")
        or_hi, or_lo = sem("or_hi"), sem("or_lo")
        wo_psum = sem("wo_psum")
        x1_ready = sem("x1_ready")
        wo_read = sem("wo_read")
        gate_psum, up_psum = sem("gate_psum"), sem("up_psum")
        silu_done = sem("silu_done")
        clip_done = sem("clip_done")
        abs_done = sem("abs_done")
        prod_done = sem("prod_done")
        interq_ready = sem("interq_ready")
        down_psum = sem("down_psum")
        down_copied = sem("down_copied")
        y_ready = sem("y_ready")

        block = ctx.enter_context(nc.Block())
        misc_before, misc_after = misc_counts()

        def bank(i):
            return ps[:, i, :]

        SC, PVB, MXB, MI = (0, 2), 4, (5, 6), 7

        def slots(i, j):
            return (2 * i + j) * 4

        def rows(it):
            return min(P, F - it * P)

        @block.sync
        def _(sp):
            xt = x_in.rearrange("(t p) d -> t p d", p=P)
            wq = wqkvT.rearrange("(k p) f -> k p f", p=P)
            for t in range(TB):
                sp.dma_start(x[:, t, :], xt[t]).then_inc(x_loaded[t], 16)
            for k in range(KD):
                sp.dma_start(wq_raw[:, k, :], wq[k]).then_inc(wq_loaded[k], 16)
            sp.dma_start(identf[:, :], eye).then_inc(tab_loaded, 16)
            sp.dma_start(cos_sb[:, :], cosT).then_inc(tab_loaded, 16)
            sp.dma_start(sin_sb[:, :], sinT).then_inc(tab_loaded, 16)
            for t in range(TB, NT):
                sp.dma_start(x[:, t, :], xt[t]).then_inc(x_loaded[t], 16)
            sp.wait_ge(proj_done, B * NPROJ)
            sp.dma_start(wo_raw[:, :, :], woT.rearrange("(k p) n -> p k n", p=P)).then_inc(wo_loaded, 16)
            for _, step, n in body_steps():
                if step != "MT":
                    continue
                sp.wait_ge(misc_read, misc_after["MT", n])
                for h in range(G):
                    r = SLOT * (h % 2) + MROW
                    sp.dma_start(qst[n % NB][r:r + 2, h // 2, :].bitcast(F32),
                                 mt[n % 2][2 * h:2 * h + 2, :].bitcast(F32)).then_inc(mrow_sent[n % NB], 16)
            for it in range(NF):
                m = rows(it)
                if it == 0:
                    sp.wait_ge(stack_psum, 3 * ITERS)
                if it >= 1:
                    sp.wait_ge(gu_hi, it)
                    sp.wait_ge(gu_lo, it)
                for k in range(KD):
                    sp.dma_start(gu_raw[:, k, :, 0:m],
                                 wguT[k * P:(k + 1) * P, :, it * P:it * P + m]).then_inc(gu_loaded, 16)
                if it == 0:
                    sp.wait_ge(misc_read, misc_after["OT", ITERS - 1])
                if it >= 1:
                    sp.wait_ge(wd_hi, it)
                    sp.wait_ge(wd_lo, it)
                sp.dma_start(wd_raw[0][0:m, :], wdT[it * P:it * P + m, :]).then_inc(wd_loaded, 16)
            ot = out.rearrange("(t p) d -> t p d", p=P)
            for t in range(NT):
                sp.wait_ge(y_ready, t + 1)
                sp.dma_start(ot[t], x[:, t, :]).then_inc(out_stored, 16)
            sp.wait_ge(out_stored, 16 * NT)

        @block.gpsimd
        def _(pool):
            pool.memset(zerob[:, :], 0.0).then_inc(consts_ready, 1)
            pool.memset(epsc[:, :], EPS).then_inc(consts_ready, 1)
            pool.memset(ones_row[:, :], 0.0).then_inc(consts_ready, 1)
            pool.wait_ge(consts_ready, 3)
            pool.affine_select(out=maskb[:, :], in_=zerob[:, :], compare_op=ALU.is_ge, fill=NEG,
                               base=0, pattern=[[-1, P]], channel_multiplier=1).then_inc(consts_ready, 1)
            pool.affine_select(out=identb[:, :], in_=zerob[:, :], compare_op=ALU.not_equal, fill=1.0,
                               base=0, pattern=[[-1, P]], channel_multiplier=1).then_inc(consts_ready, 1)
            for i, r in enumerate((MROW, MROW + 1, SLOT + MROW, SLOT + MROW + 1)):
                pool.wait_ge(consts_ready, 5 + i)
                pool.affine_select(out=ones_row[:, :], in_=ones_row[:, :], compare_op=ALU.not_equal, fill=1.0,
                                   base=-r, pattern=[[0, 1]], channel_multiplier=1).then_inc(consts_ready, 1)
            i = 0
            for b in range(B):
                for m in range(NQK):
                    pool.wait_ge(rope_prod, 2 * (i + 1))
                    if i >= 2:
                        pool.wait_ge(qk_hi, i - 1)
                        pool.wait_ge(qk_lo, i - 1)
                    pool.tensor_tensor(rope_r[i % 2][:, :], rope_u[i % 2][:, :], rope_v[i % 2][:, :],
                                   ALU.add).then_inc(rope_sum, 1)
                    i += 1
            pool.wait_ge(proj_done, B * NPROJ)
            pool.wait_ge(rope_prod, 2 * B * NQK)
            pool.wait_ge(rope_sum, B * NQK)
            for i in range(NB):
                pool.memset(kst[i][:, :, :].bitcast(F32), 0.0).then_inc(kzero_ready, 1)
            pool.wait_ge(wo_hi, 1)
            pool.tensor_tensor(wol[:, :, :], wo_raw[:, :, :], woh[:, :, :],
                                   ALU.subtract).then_inc(wo_lo, 1)
            for _, step, n in body_steps():
                if kind_of(step) != "S":
                    continue
                s = int(step[1:])
                kb, pairs = SCORE_STEPS[s]
                nq, nh = S - kb * P, 2 * len(pairs)
                pool.wait_ge(exp_done, NS * n + s + 1)
                d = probs[:, s, 0:nh * nq].rearrange("p (h q) -> p h q", q=nq)[:, :, 0:P]
                pool.affine_select(out=d, in_=d, compare_op=ALU.is_ge, fill=0.0, base=0,
                                   pattern=[[0, nh], [1, P]], channel_multiplier=-1).then_inc(masked, 1)
            for it in range(NF):
                m = rows(it)
                pool.wait_ge(gu_hi, it + 1)
                pool.tensor_tensor(gul[it % 2][:, :, :, 0:m], gu_raw[:, :, :, 0:m], guh[it % 2][:, :, :, 0:m],
                                   ALU.subtract).then_inc(gu_lo, 1)
                pool.wait_ge(wd_hi, it + 1)
                pool.tensor_tensor(wdl[0:m, it, :], wd_raw[0][0:m, :], wdh[0:m, it, :],
                                   ALU.subtract).then_inc(wd_lo, 1)

        @block.scalar
        def _(act):
            for k in range(KD):
                act.wait_ge(wq_loaded[k], 16)
                act.activation(wqh[:, k, :], wq_raw[:, k, :], ACT.Copy).then_inc(wq_hi, 1)
            act.wait_ge(consts_ready, 9)
            for b in range(B):
                act.wait_ge(var_ready, TB * (b + 1))
                act.activation(sd[:, 0, TB * b:TB * b + TB], mv[:, 0, TB * b:TB * b + TB, 1], ACT.Sqrt,
                               bias=epsc[:, 0:1]).then_inc(sd_ready, 1)
                for t in range(TB * b, TB * b + TB):
                    act.wait_ge(xt_psum, t + 1)
                    act.activation(xTh[:, :, t * P:(t + 1) * P],
                                   bank(t % 2).rearrange("p (k q) -> p k q", q=P), ACT.Copy).then_inc(xt_hi, 1)
            i = 0
            for b in range(B):
                for m in range(NPROJ):
                    if m < NQK:
                        qkh = (qkh0, qkh1)[b]
                        act.wait_ge(rope_sum, i + 1)
                        act.activation(qkh[:, m, :], rope_r[i % 2][:, :], ACT.Copy).then_inc(qk_hi, 1)
                        i += 1
                    else:
                        act.wait_ge(proj_done, NPROJ * (b + 1))
                        act.activation(vT[b][:, :], bank(2 + (NPROJ * b + m) % 4), ACT.Copy).then_inc(vt_copied, 1)
            act.wait_ge(wo_loaded, 16)
            act.activation(woh[:, :, :], wo_raw[:, :, :], ACT.Copy).then_inc(wo_hi, 1)
            act.wait_ge(kzero_ready, NB)
            for _, step, n in body_steps():
                kind = kind_of(step)
                if step in ("B0", "B1"):
                    pr = int(step[1])
                    act.wait_ge(stack_psum, 3 * n + pr + 1)
                    if n >= NB and pr == 0:
                        act.wait_ge(score_psum, NS * (n - NB + 1))
                    act.activation(qst[n % NB][:, pr, :], bank(MI), ACT.Copy).then_inc(misc_read, 1)
                elif step == "B2":
                    act.wait_ge(stack_psum, 3 * n + 3)
                    act.activation(kst[n % NB][0:SLOT, 0, :], ps[0:SLOT, MI, :], ACT.Identity,
                                   bias=ones_row[0:SLOT, 0:1]).then_inc(misc_read, 1)
                elif step == "MT":
                    act.wait_ge(mt_psum, n + 1)
                    if n >= 2:
                        act.wait_ge(mrow_sent[(n - 2) % NB], 16 * G * ((n - 2) // NB + 1))
                    act.activation(mt[n % 2][:, :], ps[0:2 * G, MI, :], ACT.Copy).then_inc(misc_read, 1)
                elif kind == "S":
                    s = int(step[1:])
                    kb, pairs = SCORE_STEPS[s]
                    nq, nh = S - kb * P, 2 * len(pairs)
                    act.wait_ge(score_psum, NS * n + s + 1)
                    if n >= 1:
                        act.wait_ge(pv_done, TB * (n - 1) + kb + 1)
                    b0 = SC[s % 2]
                    if kb < 2:
                        src = ps[:, b0:b0 + 2, 0:nq]
                    elif kb == 2:
                        src = ps[:, b0:b0 + 2, :]
                    else:
                        src = ps[:, b0, :]
                    dst = probs[:, s, 0:nh * nq]
                    if kb < 3:
                        dst = dst.rearrange("p (a q) -> p a q", a=2)
                    act.activation(dst, src, ACT.Exp, scale=float(SCALE)).then_inc(exp_done, 1)
                elif step == "PV3":
                    act.wait_ge(pv_done, TB * (n + 1))
                    if n >= 2:
                        act.wait_ge(ot_psum, n - 1)
                    act.activation(ots[n % 2][:, :], bank(PVB), ACT.Copy).then_inc(ot_copied, 1)
            act.wait_ge(misc_read, misc_after["OT", ITERS - 1])
            for t in range(NT + 3):
                if t < NT:
                    act.wait_ge(or_psum, t + 1)
                    if t >= 2:
                        act.wait_ge(wo_psum, t - 1)
                    act.activation(oth[t % 2][:, :, :], bank(t % 2).rearrange("p (k q) -> p k q", q=P),
                                   ACT.Copy).then_inc(or_hi, 1)
                if 1 <= t <= NT:
                    u = t - 1
                    act.wait_ge(var_ready, NT + 2 * u + 1)
                    act.activation(sd[:, 1, u:u + 1], mv[:, 1, u, 1:2], ACT.Sqrt,
                                   bias=epsc[:, 0:1]).then_inc(sd_ready, 1)
                    act.wait_ge(var_ready, NT + 2 * u + 2)
                    act.activation(sd[:, 2, u:u + 1], mv[:, 2, u, 1:2], ACT.Sqrt,
                                   bias=epsc[:, 0:1]).then_inc(sd_ready, 1)
                if t >= 3:
                    u = t - 3
                    act.wait_ge(xt_psum, NT + u + 1)
                    act.activation(xTh[:, :, u * P:(u + 1) * P],
                                   bank(4 + u % 2).rearrange("p (k q) -> p k q", q=P),
                                   ACT.Copy).then_inc(xt_hi, 1)
            def split_hi(it):
                m = rows(it)
                act.wait_ge(gu_loaded, 16 * KD * (it + 1))
                if it >= 2:
                    act.wait_ge(up_psum, 2 * (it - 2) + 2)
                act.activation(guh[it % 2][:, :, :, 0:m], gu_raw[:, :, :, 0:m], ACT.Copy).then_inc(gu_hi, 1)
                act.wait_ge(wd_loaded, 16 * (it + 1))
                act.activation(wdh[0:m, it, :], wd_raw[0][0:m, :], ACT.Copy).then_inc(wd_hi, 1)

            split_hi(0)
            split_hi(1)
            for u in range(2 * NF):
                it, b = u // 2, u % 2
                m = rows(it)
                f = ftmp[u % 2]
                g0 = (6, 0)[u % 2]
                act.wait_ge(gate_psum, u + 1)
                if u >= 2:
                    act.wait_ge(prod_done, u - 1)
                act.activation(f["silu"][0:m, :], ps[0:m, g0, :], ACT.Silu,
                               scale=1.0 / IN_SCALE).then_inc(silu_done, 1)
                act.wait_ge(clip_done, u + 1)
                if u >= 2:
                    act.wait_ge(interq_ready, u - 1)
                act.activation(f["absv"][0:m, :], f["clip"][0:m, :], ACT.Abs).then_inc(abs_done, 1)
                act.activation(f["sign"][0:m, :], f["clip"][0:m, :], ACT.Sign).then_inc(abs_done, 1)
                if b == 1 and it + 2 < NF:
                    split_hi(it + 2)
            for t in range(NT + 1):
                if t < NT:
                    u = 2 * NF + t
                    f = ftmp[u % 2]
                    act.wait_ge(down_psum, t + 1)
                    if t < 2:
                        act.wait_ge(clip_done, 2 * NF)
                    else:
                        act.wait_ge(clip_done, u - 1)
                    act.activation(f["y"][:, :], bank(2 + t % 4), ACT.Copy, scale=OUT_SCALE).then_inc(down_copied, 1)
                    act.wait_ge(clip_done, u + 1)
                    act.wait_ge(interq_ready, u - 1)
                    act.activation(f["absv"][:, :], f["clip"][:, :], ACT.Abs).then_inc(abs_done, 1)
                    act.activation(f["sign"][:, :], f["clip"][:, :], ACT.Sign).then_inc(abs_done, 1)
                if t >= 1:
                    v = t - 1
                    act.wait_ge(var_ready, 3 * NT + v + 1)
                    act.activation(sd[:, 3, v:v + 1], mv[:, 3, v, 1:2], ACT.Sqrt,
                                   bias=epsc[:, 0:1]).then_inc(sd_ready, 1)

        @block.vector
        def _(dve):
            count = [0]

            def link(ins):
                count[0] += 1
                ins.then_inc(dve_step, 1)
                dve.wait_ge(dve_step, count[0])

            def norm_stats(norm, t, src):
                link(dve.bn_stats(stats[:, t, :], src))
                dve.bn_aggr(mv[:, norm, t, :], stats[:, t, :]).then_inc(var_ready, 1)

            def xt_low(t, first_bank, done):
                dve.wait_ge(xt_hi, done + 1)
                cols = slice(t * P, (t + 1) * P)
                dve.tensor_tensor(xTl[:, :, cols], bank(first_bank + t % 2).rearrange("p (k q) -> p k q", q=P),
                                  xTh[:, :, cols], ALU.subtract).then_inc(xt_lo, 1)

            dve.memset(selqh[:, :, :, :].bitcast(F32), 0.0).then_inc(sel_ready, 1)
            dve.memset(selql[:, :, :, :].bitcast(F32), 0.0).then_inc(sel_ready, 1)
            dve.memset(selkh[:, :, :, :, :].bitcast(F32), 0.0).then_inc(sel_ready, 1)
            dve.memset(selkl[:, :, :, :, :].bitcast(F32), 0.0).then_inc(sel_ready, 1)
            dve.memset(vone[:, :, :, HD:32], 1.0).then_inc(sel_ready, 1)

            for b in range(B):
                for t in range(TB * b, TB * b + TB):
                    dve.wait_ge(x_loaded[t], 16)
                    norm_stats(0, t, x[:, t, :])
                dve.wait_ge(sd_ready, b + 1)
                link(dve.reciprocal(rstd[:, 0, TB * b:TB * b + TB], sd[:, 0, TB * b:TB * b + TB]))
                for t in range(TB * b, TB * b + TB):
                    if t >= 2:
                        dve.wait_ge(xt_psum, t - 1)
                    dve.tensor_scalar(xn[t % 2][:, :], x[:, t, :], mv[:, 0, t, 0:1], rstd[:, 0, t:t + 1],
                                      ALU.subtract, ALU.mult).then_inc(xn_ready, 1)
                    if t > TB * b:
                        xt_low(t - 1, 0, t - 1)
                xt_low(TB * b + TB - 1, 0, TB * b + TB - 1)
                if b == 0:
                    for k in range(KD):
                        dve.wait_ge(wq_hi, k + 1)
                        dve.tensor_tensor(wql[:, k, :], wq_raw[:, k, :], wqh[:, k, :],
                                          ALU.subtract).then_inc(wq_lo, 1)
                    dve.wait_ge(tab_loaded, 48)
                    dve.wait_ge(sel_ready, 5)
                    eye8 = identf[:, :].rearrange("p (g d) -> p g d", d=HD)
                    for slot in (0, 1):
                        dve.tensor_copy(selqh[:, :, slot, :], eye8).then_inc(sel_ready, 1)
                    dve.tensor_copy(selql[:, :, 2, :], eye8).then_inc(sel_ready, 1)
                    for ab in range(2):
                        dve.tensor_copy(selkh[:, :, ab, 0, :], eye8).then_inc(sel_ready, 1)
                        dve.tensor_copy(selkh[:, :, ab, 2, :], eye8).then_inc(sel_ready, 1)
                        dve.tensor_copy(selkl[:, :, ab, 1, :], eye8).then_inc(sel_ready, 1)
            swap = [(p & 16) | ((p + HD // 2) & 15) for p in range(32)]
            i = 0

            def qk_low(i):
                b, m = i // NQK, i % NQK
                dve.wait_ge(qk_hi, i + 1)
                dve.tensor_tensor((qkl0, qkl1)[b][:, m, :], rope_r[i % 2][:, :], (qkh0, qkh1)[b][:, m, :],
                                  ALU.subtract).then_inc(qk_lo, 1)

            for b in range(B):
                for m in range(NQK):
                    c = NPROJ * b + m
                    dve.wait_ge(proj_done, c + 1)
                    if i >= 2:
                        dve.wait_ge(rope_sum, i - 1)
                    src = bank(2 + c % 4)
                    dve.stream_shuffle(rope_s[i % 2][:, :], src, swap).then_inc(shuf_done, 1)
                    dve.tensor_tensor(rope_u[i % 2][:, :], src, cos_sb[:, :], ALU.mult).then_inc(rope_prod, 1)
                    dve.wait_ge(shuf_done, i + 1)
                    dve.tensor_tensor(rope_v[i % 2][:, :], rope_s[i % 2][:, :], sin_sb[:, :],
                                      ALU.mult).then_inc(rope_prod, 1)
                    if i >= 1:
                        qk_low(i - 1)
                    i += 1
                dve.wait_ge(v_psum, b + 1)
                dve.tensor_copy(vone[:, TB * b:TB * b + TB, :, 0:HD],
                                bank(6).rearrange("p (t g d) -> p t g d", t=TB, d=HD)).then_inc(v_ready, 1)
            qk_low(i - 1)

            dve.wait_ge(kzero_ready, NB)
            dve.wait_ge(consts_ready, 9)
            for _, step, n in body_steps():
                kind = kind_of(step)
                if kind == "M":
                    s = int(step[1:])
                    i, heads, nk = MAX_STEPS[s]
                    dve.wait_ge(max_psum, NM * n + s + 1)
                    if s == 0 and n >= 2:
                        dve.wait_ge(max_split, 2 * (n - 1))
                    src = bank(MXB[(NM * n + s) % 2])[:, 0:len(heads) * nk]
                    dve.tensor_reduce(mx[n % 2][:, i, heads[0]:heads[-1] + 1],
                                      src.rearrange("p (h k) -> p h k", k=nk), AX.X, ALU.max,
                                      negate=True).then_inc(max_red, 1)
                    if s == NM - 1:
                        dve.wait_ge(max_red, NM * (n + 1))
                        if n >= 2:
                            dve.wait_ge(mt_psum, n - 1)
                        dve.tensor_copy(ms[n % 2][:, :, :, 0], mx[n % 2][:, :, :]).then_inc(max_split, 1)
                        dve.wait_ge(max_split, 2 * n + 1)
                        dve.tensor_tensor(ms[n % 2][:, :, :, 1], mx[n % 2][:, :, :], ms[n % 2][:, :, :, 0],
                                          ALU.subtract).then_inc(max_split, 1)
                elif step == "B2":
                    dve.wait_ge(stack_psum, 3 * n + 3)
                    if n >= NB:
                        dve.wait_ge(score_psum, NS * (n - NB + 1))
                    dve.tensor_scalar(kst[n % NB][SLOT:P, 1, :], ps[SLOT:P, MI, :], ones_row[SLOT:P, 0:1], None,
                                      ALU.add).then_inc(misc_read, 1)
                elif step == "OT":
                    b, g = n // NKV, n % NKV
                    dve.wait_ge(ot_psum, n + 1)
                    o4 = bank(MI).rearrange("p (i h d) -> p i h d", i=TB, d=32)
                    dve.reciprocal(rden[n % 2][:, :, :], o4[:, :, :, HD]).then_inc(rden_ready, 1)
                    dve.wait_ge(rden_ready, n + 1)
                    dst = o_nat[:, TB * b:TB * b + TB, g * G * HD:(g + 1) * G * HD]
                    dve.tensor_tensor(dst.rearrange("p i (h d) -> p i h d", d=HD), o4[:, :, :, 0:HD],
                                      rden[n % 2][:, :, :].unsqueeze(3).broadcast_to([P, TB, G, HD]),
                                      ALU.mult).then_inc(misc_read, 1)

            dve.wait_ge(misc_read, misc_after["OT", ITERS - 1])
            for t in range(NT + 3):
                if t < NT:
                    dve.wait_ge(or_hi, t + 1)
                    dve.tensor_tensor(otl[t % 2][:, :, :], bank(t % 2).rearrange("p (k q) -> p k q", q=P),
                                      oth[t % 2][:, :, :], ALU.subtract).then_inc(or_lo, 1)
                if 1 <= t <= NT:
                    u = t - 1
                    src = bank(2 + u % 2)
                    dve.wait_ge(wo_psum, u + 1)
                    norm_stats(1, u, src)
                    dve.wait_ge(sd_ready, B + 2 * u + 1)
                    link(dve.reciprocal(rstd[:, 1, u:u + 1], sd[:, 1, u:u + 1]))
                    dve.tensor_scalar(tmp[:, :], src, mv[:, 1, u, 0:1], rstd[:, 1, u:u + 1],
                                      ALU.subtract, ALU.mult).then_inc(wo_read, 1)
                    dve.wait_ge(wo_read, u + 1)
                    dve.tensor_tensor(x[:, u, :], x[:, u, :], tmp[:, :], ALU.add).then_inc(x1_ready, 1)
                    dve.wait_ge(x1_ready, u + 1)
                    norm_stats(2, u, x[:, u, :])
                    dve.wait_ge(sd_ready, B + 2 * u + 2)
                    link(dve.reciprocal(rstd[:, 2, u:u + 1], sd[:, 2, u:u + 1]))
                    if u >= 2:
                        dve.wait_ge(xt_psum, NT + u - 1)
                    dve.tensor_scalar(xn2[u % 2][:, :], x[:, u, :], mv[:, 2, u, 0:1], rstd[:, 2, u:u + 1],
                                      ALU.subtract, ALU.mult).then_inc(xn_ready, 1)
                if t >= 3:
                    xt_low(t - 3, 4, NT + t - 3)

            def clip_to_int8(u, m):
                f = ftmp[u % 2]
                if u >= 2:
                    dve.wait_ge(abs_done, 2 * (u - 1))
                dve.tensor_scalar(f["clip"][0:m, :], f["y"][0:m, :], 127.0, -128.0, ALU.min,
                                  ALU.max).then_inc(clip_done, 1)

            def truncate(u, m, dst):
                f = ftmp[u % 2]
                dve.wait_ge(abs_done, 2 * (u + 1))
                link(dve.tensor_scalar(f["rnd"][0:m, :], f["absv"][0:m, :], MAGIC, MAGIC, ALU.add, ALU.subtract))
                link(dve.tensor_tensor(f["above"][0:m, :], f["rnd"][0:m, :], f["absv"][0:m, :], ALU.is_gt))
                link(dve.tensor_tensor(f["flo"][0:m, :], f["rnd"][0:m, :], f["above"][0:m, :], ALU.subtract))
                dve.tensor_tensor(dst, f["flo"][0:m, :], f["sign"][0:m, :], ALU.mult).then_inc(interq_ready, 1)

            for u in range(2 * NF + 1):
                if u < 2 * NF:
                    it, b = u // 2, u % 2
                    m = rows(it)
                    f = ftmp[u % 2]
                    dve.wait_ge(silu_done, u + 1)
                    dve.wait_ge(up_psum, u + 1)
                    dve.scalar_tensor_tensor(out=f["y"][0:m, :], in0=f["silu"][0:m, :], scalar=1.0,
                                             in1=ps[0:m, (7, 1)[u % 2], :], op0=ALU.mult,
                                             op1=ALU.mult).then_inc(prod_done, 1)
                    dve.wait_ge(prod_done, u + 1)
                    clip_to_int8(u, m)
                if u >= 1:
                    v = u - 1
                    m = rows(v // 2)
                    truncate(v, m, interq[0:m, v // 2, (v % 2) * S:(v % 2 + 1) * S])

            for t in range(NT + 1):
                if t < NT:
                    dve.wait_ge(down_copied, t + 1)
                    clip_to_int8(2 * NF + t, P)
                if t >= 1:
                    v = t - 1
                    u = 2 * NF + v
                    f = ftmp[u % 2]
                    truncate(u, P, f["silu"][:, :])
                    dve.wait_ge(interq_ready, u + 1)
                    norm_stats(3, v, f["silu"][:, :])
                    dve.wait_ge(sd_ready, B + 2 * NT + v + 1)
                    link(dve.reciprocal(rstd[:, 3, v:v + 1], sd[:, 3, v:v + 1]))
                    link(dve.tensor_scalar(tmp[:, :], f["silu"][:, :], mv[:, 3, v, 0:1], rstd[:, 3, v:v + 1],
                                           ALU.subtract, ALU.mult))
                    dve.tensor_tensor(x[:, v, :], x[:, v, :], tmp[:, :], ALU.add).then_inc(y_ready, 1)

        @block.tensor
        def _(pe):
            def transpose_tile(dst_bank, src, signal):
                for k in range(KD):
                    ins = pe.transpose(dst_bank[:, k * P:(k + 1) * P], src[:, k * P:(k + 1) * P], identf[:, :])
                ins.then_inc(signal, 1)

            def transpose_xn(t):
                pe.wait_ge(xn_ready, t + 1)
                if t >= 2:
                    pe.wait_ge(xt_lo, t - 1)
                transpose_tile(bank(t % 2), xn[t % 2][:, :], xt_psum)

            pe.wait_ge(tab_loaded, 48)
            for t in range(TB):
                transpose_xn(t)
            for b in range(B):
                pe.wait_ge(xt_lo, TB * (b + 1))
                for m in range(NPROJ):
                    c = NPROJ * b + m
                    if c >= 4:
                        o = c - 4
                        if o % NPROJ < NQK:
                            pe.wait_ge(rope_prod, 2 * (o - o // NPROJ + 1))
                        else:
                            pe.wait_ge(vt_copied, o // NPROJ + 1)
                    n = 0
                    for w, xx in ((wqh, xTh), (wqh, xTl), (wql, xTh)):
                        for k in range(KD):
                            if c == 0:
                                pe.wait_ge(wq_lo if w is wql else wq_hi, k + 1)
                            ins = pe.matmul(bank(2 + c % 4), w[:, k, m * P:(m + 1) * P],
                                            xx[:, k, b * S:(b + 1) * S], start=(n == 0), stop=(n == 3 * KD - 1))
                            n += 1
                    ins.then_inc(proj_done, 1)
                    if b == 0 and m == 1:
                        for t in range(TB, NT):
                            transpose_xn(t)
                pe.wait_ge(vt_copied, b + 1)
                if b >= 1:
                    pe.wait_ge(v_ready, b)
                transpose_tile(bank(6), vT[b][:, :], v_psum)

            pe.wait_ge(qk_lo, B * NQK)
            pe.wait_ge(v_ready, B)
            pe.wait_ge(sel_ready, 14)
            pe.wait_ge(consts_ready, 9)
            for _, step, n in body_steps():
                kind = kind_of(step)
                b, g = n // NKV, n % NKV
                qkh, qkl = ((qkh0, qkl0), (qkh1, qkl1))[b]
                q, kk = qst[n % NB], kst[n % NB]
                if step in MISC:
                    pe.wait_ge(misc_read, misc_before[step, n])
                if kind == "B":
                    if step == "B2":
                        sh, sl, m = selkh[:, g, :, :, :], selkl[:, g, :, :, :], NQK - 1
                        sh, sl = (w.rearrange("p a s d -> p (a s d)") for w in (sh, sl))
                    else:
                        h = G * g + 2 * int(step[1])
                        m, r = h // 8, h % 8
                        sh, sl = (w[:, r:r + 2, :, :].rearrange("p a s d -> p (a s d)") for w in (selqh, selql))
                    pe.matmul(bank(MI), sh, qkh[:, m, :], start=True, stop=False)
                    pe.matmul(bank(MI), sl, qkl[:, m, :], start=False, stop=True).then_inc(stack_psum, 1)
                elif kind == "M":
                    s = int(step[1:])
                    i, heads, nk = MAX_STEPS[s]
                    c = NM * n + s
                    pe.wait_ge(misc_read, misc_after["B2", n])
                    if c >= 2:
                        pe.wait_ge(max_red, c - 1)
                    o = bank(MXB[c % 2])
                    qs = slice(i * P, (i + 1) * P)
                    if i == 0:
                        for pr in range(NPAIR):
                            pe.matmul(o[:, pr * 2 * P:(pr + 1) * 2 * P], q[:, pr, qs], kk[:, :, 0:nk],
                                      start=(pr == 0), stop=False, skip_group_check=True)
                    elif i == 1:
                        pe.matmul(o, q[:, heads[0] // 2, qs], kk[:, :, 0:nk], start=True, stop=False,
                                  skip_group_check=True)
                    else:
                        h = heads[0]
                        pe.matmul(o[:, 0:nk], q[:, h // 2, qs], kk[:, h % 2, 0:nk], start=True, stop=False,
                                  skip_group_check=True)
                    nh = len(heads)
                    diag = o[:, 0:nh * nk].rearrange("p (h k) -> p h k", k=nk)[:, :, nk - P:nk]
                    pe.matmul(diag, identb[:, :], maskb[:, :].unsqueeze(1).broadcast_to([P, nh, P]),
                              start=False, stop=True, skip_group_check=True).then_inc(max_psum, 1)
                elif step == "MT":
                    pe.wait_ge(max_split, 2 * (n + 1))
                    for i in range(TB):
                        ins = pe.transpose(ps[0:2 * G, MI, i * P:(i + 1) * P],
                                           ms[n % 2][:, i, :, :].rearrange("p h a -> p (h a)").bitcast(F32),
                                           identf[:, :])
                    ins.then_inc(mt_psum, 1)
                elif kind == "S":
                    s = int(step[1:])
                    kb, pairs = SCORE_STEPS[s]
                    c = NS * n + s
                    if s == 0:
                        pe.wait_ge(mrow_sent[n % NB], 16 * G * (n // NB + 1))
                    if c >= 2:
                        pe.wait_ge(exp_done, c - 1)
                    b0 = SC[s % 2]
                    qs = slice(kb * P, S)
                    nq = S - kb * P
                    for ab in range(2):
                        w = kk[:, ab, kb * P:(kb + 1) * P]
                        if kb < 2:
                            o = ps[:, b0 + ab, 0:nq]
                            r = q[:, pairs[0], qs]
                        elif kb == 2:
                            o = ps[:, b0 + ab, :].rearrange("p (a q) -> p a q", q=nq)
                            r = q[:, :, qs]
                        else:
                            o = ps[:, b0, ab * 2 * nq:(ab + 1) * 2 * nq].rearrange("p (a q) -> p a q", q=nq)
                            r = q[:, :, qs]
                        ins = pe.matmul(o, w, r, start=True, stop=True, skip_group_check=True)
                    ins.then_inc(score_psum, 1)
                elif kind == "PV":
                    kb = int(step[2:])
                    nq = S - kb * P
                    pe.wait_ge(masked, NS * n + (2, 4, 5, 6)[kb])
                    if kb == 0 and n >= 1:
                        pe.wait_ge(ot_copied, n)
                    for h in range(G):
                        pr, ab = h // 2, h % 2
                        if kb < 2:
                            s, at_ = 2 * kb + pr, ab * nq
                        else:
                            s, at_ = kb + 2, (2 * ab + pr) * nq
                        ins = pe.matmul(ps[32 * h:32 * h + HD + 1, PVB, kb * P:S],
                                        vone[:, TB * b + kb, g, 0:HD + 1], probs[:, s, at_:at_ + nq],
                                        start=(kb == 0), stop=(kb == TB - 1), skip_group_check=True)
                    ins.then_inc(pv_done, 1)
                elif step == "OT":
                    pe.wait_ge(ot_copied, n + 1)
                    transpose_tile(bank(MI), ots[n % 2][:, :], ot_psum)

            for t in range(NT + 3):
                if t < NT:
                    if t == 0:
                        pe.wait_ge(misc_read, misc_after["OT", ITERS - 1])
                    if t >= 2:
                        pe.wait_ge(or_lo, t - 1)
                    transpose_tile(bank(t % 2), o_nat[:, t, :], or_psum)
                if 1 <= t <= NT:
                    u = t - 1
                    pe.wait_ge(or_lo, u + 1)
                    if u == 0:
                        pe.wait_ge(wo_lo, 1)
                    if u >= 2:
                        pe.wait_ge(wo_read, u - 1)
                    n = 0
                    for a, w in ((oth, woh), (oth, wol), (otl, woh)):
                        for k in range(KD):
                            ins = pe.matmul(bank(2 + u % 2), a[u % 2][:, k, :], w[:, k, :], start=(n == 0),
                                            stop=(n == 3 * KD - 1))
                            n += 1
                    ins.then_inc(wo_psum, 1)
                if t >= 3:
                    u = t - 3
                    pe.wait_ge(xn_ready, NT + u + 1)
                    if u >= 2:
                        pe.wait_ge(xt_lo, NT + u - 1)
                    transpose_tile(bank(4 + u % 2), xn2[u % 2][:, :], xt_psum)

            for u in range(2 * NF):
                it, b = u // 2, u % 2
                m = rows(it)
                pe.wait_ge(gu_lo, it + 1)
                if it == 0:
                    pe.wait_ge(xt_lo, NT + TB * (b + 1))
                if u >= 2:
                    pe.wait_ge(prod_done, u - 1)
                for j, signal in ((0, gate_psum), (1, up_psum)):
                    n = 0
                    for w, xx in ((guh, xTh), (guh, xTl), (gul, xTh)):
                        for k in range(KD):
                            ins = pe.matmul(ps[0:m, (6, 0)[u % 2] + j, :], w[it % 2][:, k, j, 0:m],
                                            xx[:, k, b * S:(b + 1) * S], start=(n == 0), stop=(n == 3 * KD - 1))
                            n += 1
                    ins.then_inc(signal, 1)
            pe.wait_ge(interq_ready, 2 * NF)
            pe.wait_ge(wd_lo, NF)
            for t in range(NT):
                if t >= 4:
                    pe.wait_ge(down_copied, t - 3)
                for it in range(NF):
                    m = rows(it)
                    for w in (wdh, wdl):
                        ins = pe.matmul(bank(2 + t % 4), interq[0:m, it, t * P:(t + 1) * P], w[0:m, it, :],
                                        start=(it == 0 and w is wdh), stop=(it == NF - 1 and w is wdl))
                ins.then_inc(down_psum, 1)


def rope_tables():
    inv_freq = np.float32(1.0) / np.power(np.float32(10000.0), np.arange(0, HD, 2, dtype=np.float32) / HD)
    freqs = np.arange(S, dtype=np.float32)[:, None] * inv_freq[None, :].astype(np.float32)
    emb = np.concatenate([freqs, freqs], axis=-1)
    sign = np.where(np.arange(HD) < HD // 2, -1.0, 1.0)
    cos = np.cos(emb).astype(np.float32).T
    sin = (np.sin(emb) * sign[None, :]).astype(np.float32).T
    return np.tile(cos, (P // HD, 1)), np.tile(sin, (P // HD, 1))


def kernel(L0_attn_hidden_states, L0_attn_Wq, L0_attn_Wk, L0_attn_Wv, L0_attn_Wo, L0_ffn_w_gate,
           L0_ffn_w_up, L0_ffn_w_down):
    import concourse.bacc as bacc
    from concourse.bass_utils import run_bass_kernel_spmd

    cos, sin = rope_tables()
    arrays = {
        "x": np.asarray(L0_attn_hidden_states).reshape(TOK, D),
        "wqkvT": np.concatenate([np.asarray(w).T for w in (L0_attn_Wq, L0_attn_Wk, L0_attn_Wv)], axis=1),
        "woT": np.asarray(L0_attn_Wo).T,
        "wguT": np.stack([np.asarray(L0_ffn_w_gate).T, np.asarray(L0_ffn_w_up).T], axis=1),
        "wdT": np.asarray(L0_ffn_w_down).T,
        "cosT": cos,
        "sinT": sin,
        "eye": np.eye(P, dtype=np.float32),
    }
    arrays = {k: np.ascontiguousarray(a) for k, a in arrays.items()}
    nc = bacc.Bacc("TRN2", target_bir_lowering=False, num_devices=1)
    aps = [nc.dram_tensor(k, a.shape, mybir.dt.from_np(a.dtype), kind="ExternalInput").ap()
           for k, a in arrays.items()]
    out = nc.dram_tensor("out", (TOK, D), F32, kind="ExternalOutput").ap()
    layer_kernel(nc, *aps, out)
    r = run_bass_kernel_spmd(nc, [arrays], core_ids=[0])
    return r.results[0]["out"].reshape(B, S, D)
```

```python
from contextlib import ExitStack

import numpy as np

import concourse.bass as bass
from concourse import mybir

F32 = mybir.dt.float32
F32R = mybir.dt.float32r
BF16 = mybir.dt.bfloat16
ALU = mybir.AluOpType
ACT = mybir.ActivationFunctionType
AX = mybir.AxisListType

P = 128
B, S, D = 2, 512, 512
TOK = B * S
NT = TOK // P
TB = S // P
KD = D // P
NH, NKV, HD = 32, 8, 16
G = NH // NKV
NPAIR = G // 2
SLOT = 64
MROW = 3 * HD
QKVW = D + 2 * NKV * HD
NQK = (D + NKV * HD) // P
NPROJ = QKVW // P
F = 1376
NF = -(-F // P)
EPS = 1e-5
IN_SCALE = 128.0
OUT_SCALE = 128.0
NEG = -1.0e38
MAGIC = 8388608.0
SCALE = 1.0 / np.sqrt(HD)
ITERS = B * NKV
PIECES = 4

MAX_STEPS = [(0, (0, 1, 2, 3), P)] + [(1, (0, 1), 2 * P), (1, (2, 3), 2 * P)] \
    + [(i, (h,), (i + 1) * P) for i in (2, 3) for h in range(G)]
SCORE_STEPS = [(kb, (pr,), (ab,)) for kb in (0, 1) for pr in range(NPAIR) for ab in range(2)] \
    + [(2, (0, 1), (0,)), (2, (0, 1), (1,)), (3, (0, 1), (0, 1))]
NM, NS = len(MAX_STEPS), len(SCORE_STEPS)
SCORES_OF = [sum(kb <= b for kb, _, _ in SCORE_STEPS) for b in range(TB)]
PROBS_AT = [sum(G * (S - k * P) for k in range(kb)) for kb in range(TB + 1)]
BODY = ["M0", "S4", "M1", "MT", "S5", "PV0", "M2", "S6", "M3", "S7", "OT", "M4", "S8", "M5", "S9", "S10",
        "M6", "PV1", "B0", "M7", "PV2", "M8", "B1", "S0", "M9", "PV3", "S1", "B2", "M10", "S2", "MS", "S3", "OC"]
LAG = {"B": 0, "M": 1, "MS": 1, "MT": 2, "S": 3, "PV": 3, "OC": 3, "OT": 4}
EARLY = ("S0", "S1", "S2", "S3")
NB = 3


def kind_of(step):
    return step if step in ("MS", "MT", "OC", "OT") else step.rstrip("0123456789")


def iteration(step, j):
    return j - LAG[kind_of(step)] + (step in EARLY)


def interleave(main, fill):
    out, done = [], 0
    for i, step in enumerate(main):
        out.append(step)
        upto = len(fill) * (i + 1) // len(main)
        out += fill[done:upto]
        done = upto
    return out + fill[done:]


def projection(b):
    out = []
    first, last = NPROJ * b, NPROJ * b + NQK
    for c in range(first, first + NPROJ):
        out += [("PJ", c, i) for i in range(PIECES)]
        out += [("RO", c, 0), ("RO", c, 1)] if c < last else [("VC", b, 0)]
        if c > first:
            out.append(("QH", c - 1, 0))
    return out + [("VT", b, 0)]


STEP_PIECES = {"NB": 3, "NC": 2, "WO": PIECES}


def pieces(names):
    out = []
    for name in names:
        step, i = name[:2], int(name[2:])
        out += [(step, i, k) for k in range(STEP_PIECES.get(step, 1))]
    return out


AFTER_0 = pieces(["OR0", "WO0", "NA0", "OR1", "EA0", "WO1", "NB0", "NA1", "EB0", "OR2", "EA1", "NC0", "WO2",
                  "NB1", "NA2", "TY0", "EB1", "OR3", "EA2", "NC1", "WO3", "NB2", "NA3", "TY1", "EB2", "EA3", "NC2",
                  "NB3", "TY2", "EB3", "NC3", "TY3"])
AFTER_1 = pieces(["OR4", "OR5", "FG0", "WO4", "NA4", "OR6", "EA4", "WO5", "NA5", "NB4", "OR7", "EA5", "EB4", "WO6",
                  "NA6", "NB5", "NC4", "FU0", "EA6", "EB5", "WO7", "TY4", "NA7", "NB6", "NC5", "EA7", "EB6", "FG2",
                  "TY5", "NB7", "NC6", "EB7", "FU2", "TY6", "NC7", "TY7"])


def schedule():
    out = [("ST", 0, 0), ("ST", 1, 0), ("LB", 0, 0), ("ST", 2, 0), ("LB", 1, 0), ("TX", 0, 0),
           ("ST", 3, 0), ("LB", 2, 0), ("WH", 0, 0), ("TX", 1, 0), ("LB", 3, 0), ("WH", 1, 0), ("TX", 2, 0),
           ("WH", 2, 0), ("TX", 3, 0), ("WH", 3, 0)]
    out += [("WL", k, 0) for k in range(KD)] + [("ST", t, 0) for t in range(TB, NT)]
    first = projection(0)
    begin = first.index(("QH", 1, 0)) + 1
    out += first[:begin] + [("SE", 0, 0)]
    fill = first[begin:]
    left = len(fill)
    fill += [s for t in range(TB, NT) for s in (("LB", t, 0), ("TX", t, 0))] + projection(1)
    fill.insert(fill.index(("VC", 1, 0)), ("WR", 0, 0))
    split_wo = [("WS", 0, k) for k in range(KD)]
    quota = {0: left // 2, 1: left - left // 2, 2: 12, 3: 9, 4: 9, 5: 7, 6: 7, 7: 9}
    post = AFTER_0 + [("GW", it, k) for it in range(2) for k in range(KD)]
    for j in range(ITERS + max(LAG.values())):
        main = [(step, iteration(step, j), 0) for step in BODY if 0 <= iteration(step, j) < ITERS]
        if j == NKV + LAG["OT"]:
            fill = fill + split_wo + post
            quota.update({jj: 11 for jj in range(j, 30)})
        n = min(quota.get(j, 4), len(fill))
        out += interleave(main, fill[:n])
        fill = fill[n:]
    out += fill
    out += AFTER_1
    return out


UNITS = [0, 2, 1, 3] + list(range(4, 2 * NF))



def last_use(it):
    return UNITS.index(2 * it + 1) + 1


def bank_of(step, i):
    if step == "TX":
        return 4 + i if i < TB else 7
    if step == "PJ":
        return i % 4 if i < NPROJ else 7
    if step in ("OT", "MT", "B0", "B1", "B2"):
        return 6
    if step == "VT" or i < TB:
        return 7
    return {"OR": 6 + i % 2, "WO": 4 + i % 2, "TY": 6 + i % 2}[step]


BANKED = ("TX", "PJ", "VT", "OT", "MT", "B0", "B1", "B2", "OR", "WO", "TY")


def bank_counts(steps):
    before, after, done = {}, {}, [0] * 8
    for step, i, piece in steps:
        if step in BANKED and piece == 0:
            k = bank_of(step, i)
            before[step, i] = done[k]
            done[k] += 2 if step == "B2" else 1
            after[step, i] = done[k]
    return before, after


def layer_kernel(nc, x_in, wqkvT, woT, wguT, wdT, cosT, sinT, eye, out):
    with ExitStack() as ctx:
        at = [16512]

        def place(name, shape, dt, offset=None):
            size = 4 if dt in (F32, F32R) else 2
            nbytes = int(np.prod(shape[1:])) * size
            if offset is None:
                offset = at[0]
                at[0] += -(-nbytes // 32) * 32
            return nc.alloc_sbuf_tensor_at(name, shape, dt, offset=offset), offset + nbytes

        def sem(name):
            return ctx.enter_context(nc.semaphore(name))

        x, _ = place("x", [P, NT, D], F32)
        xh = [place(f"xh{b}", [P, KD, S], F32R)[0] for b in range(B)]
        xl = [place(f"xl{b}", [P, KD, S], F32R)[0] for b in range(B)]
        a_xl1 = at[0] - 4 * KD * S
        a_wo = at[0]
        woh, _ = place("woh", [P, KD, D], F32R)
        wol, _ = place("wol", [P, KD, D], F32R)
        a_o1 = at[0]
        o = [None] * B
        o[1], a_o0 = place("o1", [P, TB, D], F32)
        o[0], _ = place("o0", [P, TB, D], F32)
        a_g = at[0]
        qkh, qkl = [None] * B, [None] * B
        qkh[0], _ = place("qkh0", [P, NQK, S], F32R)
        qkl[0], _ = place("qkl0", [P, NQK, S], F32R)
        a_r2 = at[0]
        qkh[1], _ = place("qkh1", [P, NQK, S], F32R)
        qkl[1], _ = place("qkl1", [P, NQK, S], F32R)
        vone, _ = place("vone", [P, NT, NKV, 32], F32)
        cos_sb, _ = place("cos_sb", [P, S], F32)
        sin_sb, _ = place("sin_sb", [P, S], F32)
        selqh, _ = place("selqh", [P, 8, 4, HD], F32R)
        selql, _ = place("selql", [P, 8, 4, HD], F32R)
        selkh, _ = place("selkh", [P, NKV, 2, 4, HD], F32R)
        selkl, _ = place("selkl", [P, NKV, 2, 4, HD], F32R)
        a_r1 = at[0]
        qst = [place(f"qst{i}", [P, NPAIR, S], F32R)[0] for i in range(NB)]
        kst = [place(f"kst{i}", [P, 2, S], F32R)[0] for i in range(NB)]
        a_probs = at[0]
        probs, _ = place("probs", [P, PROBS_AT[-1]], F32)
        a_e = at[0]
        ots, _ = place("ots", [P, S], F32)
        mt, _ = place("mt", [2 * G, S], F32R)
        a_tmp = at[0]
        rope_u = [place(f"rope_u{i}", [P, S], F32)[0] for i in range(2)]
        rope_s = [place(f"rope_s{i}", [P, S], F32)[0] for i in range(2)]
        a_xn = at[0]
        xn = [place(f"xn{i}", [P, D], F32)[0] for i in range(2)]
        identf, _ = place("identf", [P, P], F32)
        identb, _ = place("identb", [P, P], BF16)
        maskb, _ = place("maskb", [P, P], BF16)
        zerob, _ = place("zerob", [P, P], BF16)
        ones_row, _ = place("ones_row", [P, 1], F32)
        epsc, _ = place("epsc", [P, 1], F32)
        mx = [place(f"mx{i}", [P, TB, G], F32)[0] for i in range(2)]
        ms = [place(f"ms{i}", [P, TB, G, 2], F32R)[0] for i in range(2)]
        rden = [place(f"rden{i}", [P, TB, G], F32)[0] for i in range(2)]
        stats, _ = place("stats", [P, NT, 6], F32)
        mv, _ = place("mv", [P, 4, NT, 2], F32)
        sd, _ = place("sd", [P, 4, NT], F32)
        rstd, _ = place("rstd", [P, 4, NT], F32)
        guess, _ = place("guess", [P, 4, NT], F32)
        newt, _ = place("newt", [P, 4, NT], F32)
        assert at[0] <= 229368, at[0]

        vT = xn[1]
        wq_raw, e = place("wq_raw", [P, KD, QKVW], F32, a_probs)
        assert e <= a_e
        wqh, e = place("wqh", [P, KD, QKVW], F32R, a_wo)
        wql, e = place("wql", [P, KD, QKVW], F32R, e)
        assert e <= a_o0
        wo_raw, _ = place("wo_raw", [P, KD, D], F32, a_xl1)
        oth, otl = [None] * 2, [None] * 2
        oth[0], e = place("oth0", [P, KD, P], F32R, a_tmp)
        otl[0], e = place("otl0", [P, KD, P], F32R, e)
        aw = [None] * 2
        aw[0], e = place("aw0", [P, D], F32, e)
        aw[1], e = place("aw1", [P, D], F32, e)
        oth[1], e = place("oth1", [P, KD, P], F32R, a_e)
        otl[1], e = place("otl1", [P, KD, P], F32R, e)
        xn2 = xn

        def ot_of(t):
            return 0 if t < TB else t % 2

        def xn_of(t):
            return (xn + rope_s)[t] if t < TB else xn[t % 2]

        guh, gul = [None] * 2, [None] * 2
        e = a_g
        for i in range(2):
            guh[i], e = place(f"guh{i}", [P, KD, 2, P], F32R, e)
            gul[i], e = place(f"gul{i}", [P, KD, 2, P], F32R, e)
        gu_raw, e = place("gu_raw", [P, KD, 2, P], F32, e)
        assert e <= a_r2
        wdh, e = place("wdh", [P, NF, D], F32R, a_r2)
        wdl, e = place("wdl", [P, NF, D], F32R, e)
        assert e <= a_r1
        wd_raw = [place(f"wd_raw{i}", [P, D], F32, a_wo + 4 * D * i)[0] for i in range(2)]
        interq, e = place("interq", [P, NF, TOK], F32R, a_r1)
        assert e <= a_e
        ftmp = []
        for i, a in ((0, a_o0), (1, a_o1)):
            names = {}
            for j, k in enumerate(("y", "absv", "sign", "rnd")):
                names[k] = place(f"f{i}_{k}", [P, S], F32, a + 4 * S * j)[0]
            names["above"] = place(f"f{i}_above", [P, S], F32, a_e + 4 * S * i)[0]
            ftmp.append(names)

        ps = ctx.enter_context(nc.psum_tensor("ps", [P, 8, 512], F32))
        SC, PVB, MXB, MI = (0, 1, 2), 3, (4, 5), 6
        FFB = ((0, 1), (2, 3))
        DNB = (4, 5, 6, 7)

        x_loaded = [sem(f"x_loaded{t}") for t in range(NT)]
        wq_loaded = [sem(f"wq_loaded{k}") for k in range(KD)]
        eye_loaded, rope_loaded = sem("eye_loaded"), sem("rope_loaded")
        wo_loaded = sem("wo_loaded")
        gu_loaded = [sem(f"gu_loaded{k}") for k in range(KD)]
        wd_loaded = [sem(f"wd_loaded{i}") for i in range(2)]
        out_stored = sem("out_stored")
        bank_read = [sem(f"bank_read{i}") for i in range(8)]
        consts_ready = sem("consts_ready")
        kzero_ready = sem("kzero_ready")
        sel_ready = sem("sel_ready")
        wq_hi, wq_lo = sem("wq_hi"), sem("wq_lo")
        wo_hi, wo_lo = sem("wo_hi"), sem("wo_lo")
        gu_hi, gu_lo = sem("gu_hi"), sem("gu_lo")
        wd_hi, wd_lo = sem("wd_hi"), sem("wd_lo")
        dve_step = sem("dve_step")
        act_step = sem("act_step")
        var_ready = [sem(f"var_ready{i}") for i in range(4)]
        sd_ready = [sem(f"sd_ready{i}") for i in range(4)]
        xn_ready, xn2_ready = sem("xn_ready"), sem("xn2_ready")
        xt_psum, xt2_psum = sem("xt_psum"), sem("xt2_psum")
        xt_hi, xt2_hi = sem("xt_hi"), sem("xt2_hi")
        proj_done = sem("proj_done")
        shuf_done = sem("shuf_done")
        rope_cos = sem("rope_cos")
        rope_sum = sem("rope_sum")
        qk_hi, qk_lo = sem("qk_hi"), sem("qk_lo")
        v_psum = sem("v_psum")
        stack_psum = sem("stack_psum")
        max_psum = sem("max_psum")
        max_red = sem("max_red")
        max_split = sem("max_split")
        mt_psum = sem("mt_psum")
        mrow_sent = [sem(f"mrow_sent{i}") for i in range(NB)]
        score_psum = sem("score_psum")
        exp_done = sem("exp_done")
        masked = sem("masked")
        pv_done = sem("pv_done")
        ot_copied, ot_psum = sem("ot_copied"), sem("ot_psum")
        rden_ready = sem("rden_ready")
        or_psum, or_hi = sem("or_psum"), sem("or_hi")
        wo_psum = sem("wo_psum")
        x1_ready = sem("x1_ready")
        gate_psum, up_psum = sem("gate_psum"), sem("up_psum")
        silu_done = sem("silu_done")
        prod_done = sem("prod_done")
        clip_done = sem("clip_done")
        abs_done = sem("abs_done")
        interq_ready = sem("interq_ready")
        down_psum = sem("down_psum")
        down_copied = sem("down_copied")
        y_normed = sem("y_normed")
        y_ready = sem("y_ready")
        last_ready = sem("last_ready")

        block = ctx.enter_context(nc.Block())
        steps = schedule()
        before, after = bank_counts(steps)

        def bank(i):
            return ps[:, i, :]

        def blocks(i):
            return bank(i).rearrange("p (k q) -> p k q", q=P)

        def wait_read(engine, step, i):
            engine.wait_ge(bank_read[bank_of(step, i)], after[step, i])

        def wait_free(engine, step, i):
            if before[step, i] > 0:
                engine.wait_ge(bank_read[bank_of(step, i)], before[step, i])

        def read_of(step, i):
            return bank_read[bank_of(step, i)]

        def last_read(k, names):
            return max([v for (s, i), v in after.items() if s in names and bank_of(s, i) == k] + [0])

        FIRST_USES = ("TX", "PJ", "VT")

        def weight_steps():
            for p in range(2 * NF):
                yield from weights_after(p)

        def weights_after(p):
            out = [("gu", it) for it in range(2, NF) if last_use(it - 2) == p + 1]
            return out + ([("wd", p)] if p < NF else [])

        def rows(it):
            return min(P, F - it * P)

        @block.sync
        def _(sp):
            xt = x_in.rearrange("(t p) d -> t p d", p=P)
            wq = wqkvT.rearrange("(k p) f -> k p f", p=P)
            sp.dma_start(x[:, 0, :], xt[0]).then_inc(x_loaded[0], 16)
            sp.dma_start(identf[:, :], eye).then_inc(eye_loaded, 16)
            for t in range(1, TB):
                sp.dma_start(x[:, t, :], xt[t]).then_inc(x_loaded[t], 16)
            for k in range(KD):
                sp.dma_start(wq_raw[:, k, :], wq[k]).then_inc(wq_loaded[k], 16)
            sp.dma_start(cos_sb[:, :], cosT).then_inc(rope_loaded, 16)
            sp.dma_start(sin_sb[:, :], sinT).then_inc(rope_loaded, 16)
            for t in range(TB, NT):
                sp.dma_start(x[:, t, :], xt[t]).then_inc(x_loaded[t], 16)
            for step, n, piece in steps:
                if step == "WR":
                    sp.wait_ge(proj_done, B * NPROJ)
                    sp.dma_start(wo_raw[:, :, :], woT.rearrange("(k p) n -> p k n", p=P)).then_inc(wo_loaded, 16)
                elif step == "MT":
                    wait_read(sp, "MT", n)
                    for h in range(G):
                        r = SLOT * (h % 2) + MROW
                        sp.dma_start(qst[n % NB][r:r + 2, h // 2, :].bitcast(F32),
                                     mt[2 * h:2 * h + 2, :].bitcast(F32)).then_inc(mrow_sent[n % NB], 16)
                elif step == "GW":
                    if n == 0 and piece == 0:
                        sp.wait_ge(stack_psum, 3 * NKV)
                    if n == 1:
                        sp.wait_ge(gu_lo, piece + 1)
                    m = rows(n)
                    sp.dma_start(gu_raw[:, piece, :, 0:m],
                                 wguT[piece * P:(piece + 1) * P, :, n * P:n * P + m]).then_inc(gu_loaded[piece], 16)
            for kind, it in weight_steps():
                m = rows(it)
                if kind == "gu":
                    sp.wait_ge(gu_lo, KD * it)
                    for k in range(KD):
                        sp.dma_start(gu_raw[:, k, :, 0:m],
                                     wguT[k * P:(k + 1) * P, :, it * P:it * P + m]).then_inc(gu_loaded[k], 16)
                else:
                    if it == 0:
                        sp.wait_ge(wo_psum, NT)
                    if it >= 2:
                        sp.wait_ge(wd_lo, it - 1)
                    sp.dma_start(wd_raw[it % 2][0:m, :], wdT[it * P:it * P + m, :]).then_inc(wd_loaded[it % 2], 16)
            ot = out.rearrange("(t p) d -> t p d", p=P)
            for t in range(NT):
                if t < NT - 1:
                    sp.wait_ge(y_ready, t + 1)
                else:
                    sp.wait_ge(last_ready, 1)
                sp.dma_start(ot[t], x[:, t, :]).then_inc(out_stored, 16)
            sp.wait_ge(out_stored, 16 * NT)

        @block.gpsimd
        def _(pool):
            pool.memset(epsc[:, :], EPS).then_inc(consts_ready, 1)
            pool.memset(zerob[:, :], 0.0).then_inc(consts_ready, 1)
            pool.memset(ones_row[:, :], 0.0).then_inc(consts_ready, 1)
            pool.wait_ge(consts_ready, 3)
            pool.affine_select(out=maskb[:, :], in_=zerob[:, :], compare_op=ALU.is_ge, fill=NEG,
                               base=0, pattern=[[-1, P]], channel_multiplier=1).then_inc(consts_ready, 1)
            pool.affine_select(out=identb[:, :], in_=zerob[:, :], compare_op=ALU.not_equal, fill=1.0,
                               base=0, pattern=[[-1, P]], channel_multiplier=1).then_inc(consts_ready, 1)
            for i, r in enumerate((MROW, MROW + 1, SLOT + MROW, SLOT + MROW + 1)):
                pool.wait_ge(consts_ready, 5 + i)
                pool.affine_select(out=ones_row[:, :], in_=ones_row[:, :], compare_op=ALU.not_equal, fill=1.0,
                                   base=-r, pattern=[[0, 1]], channel_multiplier=1).then_inc(consts_ready, 1)
            pool.memset(selqh[:, :, :, :].bitcast(F32), 0.0).then_inc(sel_ready, 1)
            pool.memset(selql[:, :, :, :].bitcast(F32), 0.0).then_inc(sel_ready, 1)
            pool.memset(selkh[:, :, :, :, :].bitcast(F32), 0.0).then_inc(sel_ready, 1)
            pool.memset(selkl[:, :, :, :, :].bitcast(F32), 0.0).then_inc(sel_ready, 1)
            pool.memset(vone[:, :, :, HD:32], 1.0).then_inc(sel_ready, 1)
            for i in range(NB):
                pool.memset(kst[i][:, :, :].bitcast(F32), 0.0).then_inc(kzero_ready, 1)
            for step, n, piece in steps:
                kind = kind_of(step)
                if step == "RO" and piece == 1:
                    i = n - n // NPROJ
                    wait_read(pool, "PJ", n)
                    pool.tensor_tensor(rope_u[i % 2][:, :], rope_u[i % 2][:, :], rope_s[i % 2][:, :],
                                       ALU.add).then_inc(rope_sum, 1)
                elif step == "WS":
                    pool.wait_ge(wo_hi, piece + 1)
                    pool.tensor_tensor(wol[:, piece, :], wo_raw[:, piece, :], woh[:, piece, :],
                                       ALU.subtract).then_inc(wo_lo, 1)
                elif kind == "S":
                    kb = int(SCORE_STEPS[int(step[1:])][0])
                    if int(step[1:]) != SCORES_OF[kb] - 1:
                        continue
                    nq = S - kb * P
                    pool.wait_ge(exp_done, NS * n + SCORES_OF[kb])
                    d = probs[:, PROBS_AT[kb]:PROBS_AT[kb + 1]].rearrange("p (h q) -> p h q", q=nq)[:, :, 0:P]
                    pool.affine_select(out=d, in_=d, compare_op=ALU.is_ge, fill=0.0, base=0,
                                       pattern=[[0, G], [1, P]], channel_multiplier=-1).then_inc(masked, 1)
                elif step == "GW":
                    m = rows(n)
                    pool.wait_ge(gu_hi, KD * n + piece + 1)
                    pool.tensor_tensor(gul[n][:, piece, :, 0:m], gu_raw[:, piece, :, 0:m],
                                       guh[n][:, piece, :, 0:m], ALU.subtract).then_inc(gu_lo, 1)
            for kind, it in weight_steps():
                m = rows(it)
                if kind == "gu":
                    pool.wait_ge(gu_hi, KD * (it + 1))
                    pool.tensor_tensor(gul[it % 2][:, :, :, 0:m], gu_raw[:, :, :, 0:m],
                                       guh[it % 2][:, :, :, 0:m], ALU.subtract).then_inc(gu_lo, KD)
                else:
                    pool.wait_ge(wd_hi, it + 1)
                    pool.tensor_tensor(wdl[0:m, it, :], wd_raw[it % 2][0:m, :], wdh[0:m, it, :],
                                       ALU.subtract).then_inc(wd_lo, 1)
            for t in range(NT - 1):
                pool.wait_ge(y_normed, t + 1)
                pool.tensor_tensor(x[:, t, :], x[:, t, :], ftmp[t % 2]["rnd"][:, :], ALU.add).then_inc(y_ready, 1)

        @block.scalar
        def _(act):
            linked = [0]

            def guess_rstd(norm, t):
                act.wait_ge(var_ready[norm], t + 1)
                act.activation(sd[:, norm, t:t + 1], mv[:, norm, t, 1:2], ACT.Ln,
                               bias=epsc[:, 0:1]).then_inc(act_step, 1)
                linked[0] += 1
                act.wait_ge(act_step, linked[0])
                act.activation(guess[:, norm, t:t + 1], sd[:, norm, t:t + 1], ACT.Exp,
                               scale=-0.5).then_inc(sd_ready[norm], 1)

            def root(norm, t):
                act.wait_ge(var_ready[norm], t + 1)
                act.activation(sd[:, norm, t:t + 1], mv[:, norm, t, 1:2], ACT.Sqrt,
                               bias=epsc[:, 0:1]).then_inc(sd_ready[norm], 1)

            act.wait_ge(consts_ready, 1)
            for step, n, piece in steps:
                kind = kind_of(step)
                if step == "ST":
                    root(0, n)
                    if n == NT - 1:
                        act.preload_act_table_set("natural_log_exp_and_others")
                        act.wait_ge(consts_ready, 9)
                elif step == "WH":
                    act.wait_ge(wq_loaded[n], 16)
                    act.activation(wqh[:, n, :], wq_raw[:, n, :], ACT.Copy).then_inc(wq_hi, 1)
                elif step == "TX":
                    b, tb = n // TB, n % TB
                    act.wait_ge(xt_psum, n + 1)
                    act.activation(xh[b][:, :, tb * P:(tb + 1) * P], blocks(bank_of("TX", n)),
                                   ACT.Copy).then_inc(xt_hi, 1)
                elif step == "QH":
                    b, m, i = n // NPROJ, n % NPROJ, n - n // NPROJ
                    act.wait_ge(rope_sum, i + 1)
                    act.activation(qkh[b][:, m, :], rope_u[i % 2][:, :], ACT.Copy).then_inc(qk_hi, 1)
                elif step == "VC":
                    act.wait_ge(proj_done, NPROJ * (n + 1))
                    act.wait_ge(xt_psum, TB * (n + 1))
                    if n >= 1:
                        act.wait_ge(v_psum, n)
                    last = NPROJ * n + NQK
                    act.activation(vT[:, :], bank(bank_of("PJ", last)), ACT.Copy).then_inc(read_of("PJ", last), 1)
                elif step == "WS":
                    if piece == 0:
                        act.wait_ge(wo_loaded, 16)
                    act.activation(woh[:, piece, :], wo_raw[:, piece, :], ACT.Copy).then_inc(wo_hi, 1)
                elif step in ("B0", "B1"):
                    pr = int(step[1])
                    act.wait_ge(stack_psum, 3 * n + pr + 1)
                    if n >= NB and pr == 0:
                        act.wait_ge(score_psum, NS * (n - NB + 1))
                    act.activation(qst[n % NB][:, pr, :], bank(MI), ACT.Copy).then_inc(bank_read[MI], 1)
                elif step == "B2":
                    act.wait_ge(stack_psum, 3 * n + 3)
                    if n < NB:
                        act.wait_ge(kzero_ready, n + 1)
                    act.activation(kst[n % NB][0:SLOT, 0, :], ps[0:SLOT, MI, :], ACT.Identity,
                                   bias=ones_row[0:SLOT, 0:1]).then_inc(bank_read[MI], 1)
                elif step == "MT":
                    act.wait_ge(mt_psum, n + 1)
                    if n >= 1:
                        act.wait_ge(mrow_sent[(n - 1) % NB], 16 * G * ((n - 1) // NB + 1))
                    act.activation(mt[:, :], ps[0:2 * G, MI, :], ACT.Copy).then_inc(bank_read[MI], 1)
                elif kind == "S":
                    s = int(step[1:])
                    kb, pairs, halves = SCORE_STEPS[s]
                    c, w = NS * n + s, len(pairs) * len(halves) * (S - kb * P)
                    first = PROBS_AT[kb] + sum(w for k, _, _ in SCORE_STEPS[:s] if k == kb)
                    act.wait_ge(score_psum, c + 1)
                    if n >= 1:
                        act.wait_ge(pv_done, TB * (n - 1) + kb + 1)
                    act.activation(probs[:, first:first + w], ps[:, SC[c % 3], 0:w], ACT.Exp,
                                   scale=float(SCALE)).then_inc(exp_done, 1)
                elif step == "OC":
                    act.wait_ge(pv_done, TB * (n + 1))
                    if n >= 1:
                        act.wait_ge(ot_psum, n)
                    act.activation(ots[:, :], bank(PVB), ACT.Copy).then_inc(ot_copied, 1)
                elif step == "OR":
                    if n == 0:
                        act.wait_ge(qk_lo, B * NQK)
                    if n > TB:
                        act.wait_ge(wo_psum, n - 1)
                    elif n >= 1:
                        act.wait_ge(wo_psum, n)
                    act.wait_ge(or_psum, n + 1)
                    act.activation(oth[ot_of(n)][:, :, :], blocks(bank_of("OR", n)), ACT.Copy).then_inc(or_hi, 1)
                elif step == "NA":
                    act.wait_ge(wo_psum, n + 1)
                    if n >= 2:
                        act.wait_ge(x1_ready, n - 1)
                    act.activation(aw[n % 2][:, :], bank(bank_of("WO", n)), ACT.Copy).then_inc(read_of("WO", n), 1)
                elif step == "EA":
                    guess_rstd(1, n)
                elif step == "EB":
                    guess_rstd(2, n)
                elif step == "TY":
                    b, tb = n // TB, n % TB
                    act.wait_ge(xt2_psum, n + 1)
                    act.activation(xh[b][:, :, tb * P:(tb + 1) * P], blocks(bank_of("TY", n)),
                                   ACT.Copy).then_inc(xt2_hi, 1)
                elif step == "GW":
                    m = rows(n)
                    act.wait_ge(gu_loaded[piece], 16 * (n + 1))
                    act.activation(guh[n][:, piece, :, 0:m], gu_raw[:, piece, :, 0:m], ACT.Copy).then_inc(gu_hi, 1)

            def split_gu(it):
                m = rows(it)
                for k in range(KD):
                    act.wait_ge(gu_loaded[k], 16 * (it + 1))
                act.wait_ge(up_psum, last_use(it - 2))
                act.activation(guh[it % 2][:, :, :, 0:m], gu_raw[:, :, :, 0:m], ACT.Copy).then_inc(gu_hi, KD)

            def split_wd(it):
                m = rows(it)
                act.wait_ge(wd_loaded[it % 2], 16 * (it // 2 + 1))
                act.activation(wdh[0:m, it, :], wd_raw[it % 2][0:m, :], ACT.Copy).then_inc(wd_hi, 1)

            def abs_and_sign(p, m):
                f = ftmp[p % 2]
                act.wait_ge(clip_done, p + 1)
                if p >= 2:
                    act.wait_ge(interq_ready, p - 1)
                act.activation(f["absv"][0:m, :], f["y"][0:m, :], ACT.Abs).then_inc(abs_done, 1)
                act.activation(f["sign"][0:m, :], f["y"][0:m, :], ACT.Sign).then_inc(abs_done, 1)

            for p, u in enumerate(UNITS):
                m = rows(u // 2)
                act.wait_ge(gate_psum, p + 1)
                if p >= 2:
                    act.wait_ge(abs_done, 2 * (p - 1))
                act.activation(ftmp[p % 2]["y"][0:m, :], ps[0:m, FFB[p % 2][0], :], ACT.Silu,
                               scale=1.0 / IN_SCALE).then_inc(silu_done, 1)
                abs_and_sign(p, m)
                for kind, it in weights_after(p):
                    if kind == "gu":
                        split_gu(it)
                    else:
                        split_wd(it)
            for t in range(NT + 1):
                if t < NT:
                    p = 2 * NF + t
                    act.wait_ge(down_psum, t + 1)
                    act.wait_ge(abs_done, 2 * (p - 1))
                    act.activation(ftmp[p % 2]["y"][:, :], bank(DNB[t % 4]), ACT.Copy,
                                   scale=OUT_SCALE).then_inc(down_copied, 1)
                    abs_and_sign(p, P)
                if t >= 1:
                    root(3, t - 1)

        @block.vector
        def _(dve):
            count = [0]

            def link(ins):
                count[0] += 1
                ins.then_inc(dve_step, 1)
                dve.wait_ge(dve_step, count[0])

            def norm_stats(norm, t, src):
                link(dve.bn_stats(stats[:, t, :], src))
                dve.bn_aggr(mv[:, norm, t, :], stats[:, t, :]).then_inc(var_ready[norm], 1)

            def newton(norm, t):
                dve.wait_ge(sd_ready[norm], t + 1)
                v, r, a = mv[:, norm, t, 1:2], guess[:, norm, t:t + 1], newt[:, norm, t:t + 1]
                link(dve.scalar_tensor_tensor(out=a, in0=v, scalar=EPS, in1=r, op0=ALU.add, op1=ALU.mult))
                link(dve.scalar_tensor_tensor(out=a, in0=a, scalar=-0.5, in1=r, op0=ALU.mult, op1=ALU.mult))
                link(dve.scalar_tensor_tensor(out=rstd[:, norm, t:t + 1], in0=a, scalar=1.5, in1=r,
                                              op0=ALU.add, op1=ALU.mult))

            def normalise(norm, t, dst, src):
                return dve.tensor_scalar(dst, src, mv[:, norm, t, 0:1], rstd[:, norm, t:t + 1],
                                         ALU.subtract, ALU.mult)

            swap = [(p & 16) | ((p + HD // 2) & 15) for p in range(32)]

            for step, n, piece in steps:
                kind = kind_of(step)
                if step == "ST":
                    dve.wait_ge(x_loaded[n], 16)
                    norm_stats(0, n, x[:, n, :])
                elif step == "LB":
                    dve.wait_ge(sd_ready[0], n + 1)
                    link(dve.reciprocal(rstd[:, 0, n:n + 1], sd[:, 0, n:n + 1]))
                    if n >= TB:
                        dve.wait_ge(xt_psum, max(n - 1, TB))
                    if n == TB + 1:
                        dve.wait_ge(v_psum, 1)
                    normalise(0, n, xn_of(n)[:, :], x[:, n, :]).then_inc(xn_ready, 1)
                elif step == "TX":
                    b, cols = n // TB, slice(n % TB * P, (n % TB + 1) * P)
                    dve.wait_ge(xt_hi, n + 1)
                    dve.tensor_tensor(xl[b][:, :, cols], blocks(bank_of("TX", n)), xh[b][:, :, cols],
                                      ALU.subtract).then_inc(read_of("TX", n), 1)
                elif step == "WL":
                    dve.wait_ge(wq_hi, n + 1)
                    dve.tensor_tensor(wql[:, n, :], wq_raw[:, n, :], wqh[:, n, :],
                                      ALU.subtract).then_inc(wq_lo, 1)
                elif step == "SE":
                    dve.wait_ge(eye_loaded, 16)
                    dve.wait_ge(sel_ready, 5)
                    eye8 = identf[:, :].rearrange("p (g d) -> p g d", d=HD)
                    for slot in (0, 1):
                        dve.tensor_copy(selqh[:, :, slot, :], eye8).then_inc(sel_ready, 1)
                    dve.tensor_copy(selql[:, :, 2, :], eye8).then_inc(sel_ready, 1)
                    for ab in range(2):
                        dve.tensor_copy(selkh[:, :, ab, 0, :], eye8).then_inc(sel_ready, 1)
                        dve.tensor_copy(selkh[:, :, ab, 2, :], eye8).then_inc(sel_ready, 1)
                        dve.tensor_copy(selkl[:, :, ab, 1, :], eye8).then_inc(sel_ready, 1)
                elif step == "RO":
                    i = n - n // NPROJ
                    src = bank(bank_of("PJ", n))
                    if piece == 0:
                        dve.wait_ge(proj_done, n + 1)
                        if n == 0:
                            dve.wait_ge(rope_loaded, 32)
                        if i >= 2:
                            dve.wait_ge(qk_lo, i - 1)
                        dve.stream_shuffle(rope_s[i % 2][:, :], src, swap).then_inc(shuf_done, 1)
                        dve.tensor_tensor(rope_u[i % 2][:, :], src, cos_sb[:, :], ALU.mult).then_inc(rope_cos, 1)
                    else:
                        dve.wait_ge(shuf_done, i + 1)
                        dve.wait_ge(rope_cos, i + 1)
                        dve.tensor_tensor(rope_s[i % 2][:, :], rope_s[i % 2][:, :], sin_sb[:, :],
                                          ALU.mult).then_inc(read_of("PJ", n), 1)
                elif step == "QH":
                    b, m, i = n // NPROJ, n % NPROJ, n - n // NPROJ
                    dve.wait_ge(qk_hi, i + 1)
                    dve.tensor_tensor(qkl[b][:, m, :], rope_u[i % 2][:, :], qkh[b][:, m, :],
                                      ALU.subtract).then_inc(qk_lo, 1)
                elif step == "VT":
                    dve.wait_ge(v_psum, n + 1)
                    dve.tensor_copy(vone[:, TB * n:TB * n + TB, :, 0:HD],
                                    bank(bank_of("VT", n)).rearrange("p (t g d) -> p t g d", t=TB,
                                                                     d=HD)).then_inc(read_of("VT", n), 1)
                elif kind == "M":
                    s = int(step[1:])
                    i, heads, nk = MAX_STEPS[s]
                    dve.wait_ge(max_psum, NM * n + s + 1)
                    if s == 0 and n >= 2:
                        dve.wait_ge(max_split, 2 * (n - 1))
                    src = bank(MXB[(NM * n + s) % 2])[:, 0:len(heads) * nk]
                    dve.tensor_reduce(mx[n % 2][:, i, heads[0]:heads[-1] + 1],
                                      src.rearrange("p (h k) -> p h k", k=nk), AX.X, ALU.max,
                                      negate=True).then_inc(max_red, 1)
                elif step == "MS":
                    dve.wait_ge(max_red, NM * (n + 1))
                    if n >= 2:
                        dve.wait_ge(mt_psum, n - 1)
                    dve.tensor_copy(ms[n % 2][:, :, :, 0], mx[n % 2][:, :, :]).then_inc(max_split, 1)
                    dve.wait_ge(max_split, 2 * n + 1)
                    dve.tensor_tensor(ms[n % 2][:, :, :, 1], mx[n % 2][:, :, :], ms[n % 2][:, :, :, 0],
                                      ALU.subtract).then_inc(max_split, 1)
                elif step == "B2":
                    dve.wait_ge(stack_psum, 3 * n + 3)
                    if n == 0:
                        dve.wait_ge(consts_ready, 9)
                    if n < NB:
                        dve.wait_ge(kzero_ready, n + 1)
                    else:
                        dve.wait_ge(score_psum, NS * (n - NB + 1))
                    dve.tensor_scalar(kst[n % NB][SLOT:P, 1, :], ps[SLOT:P, MI, :], ones_row[SLOT:P, 0:1], None,
                                      ALU.add).then_inc(bank_read[MI], 1)
                elif step == "OT":
                    b, g = n // NKV, n % NKV
                    dve.wait_ge(ot_psum, n + 1)
                    if n == NKV:
                        dve.wait_ge(proj_done, B * NPROJ)
                    o4 = bank(MI).rearrange("p (i h d) -> p i h d", i=TB, d=32)
                    dve.reciprocal(rden[n % 2][:, :, :], o4[:, :, :, HD]).then_inc(rden_ready, 1)
                    dve.wait_ge(rden_ready, n + 1)
                    dst = o[b][:, :, g * G * HD:(g + 1) * G * HD]
                    dve.tensor_tensor(dst.rearrange("p i (h d) -> p i h d", d=HD), o4[:, :, :, 0:HD],
                                      rden[n % 2][:, :, :].unsqueeze(3).broadcast_to([P, TB, G, HD]),
                                      ALU.mult).then_inc(bank_read[MI], 1)
                elif step == "OR":
                    dve.wait_ge(or_hi, n + 1)
                    dve.tensor_tensor(otl[ot_of(n)][:, :, :], blocks(bank_of("OR", n)), oth[ot_of(n)][:, :, :],
                                      ALU.subtract).then_inc(read_of("OR", n), 1)
                elif step == "NA":
                    wait_read(dve, "WO", n)
                    norm_stats(1, n, aw[n % 2][:, :])
                elif step == "NB":
                    if piece == 0:
                        newton(1, n)
                        link(normalise(1, n, aw[n % 2][:, :], aw[n % 2][:, :]))
                    elif piece == 1:
                        dve.tensor_tensor(x[:, n, :], x[:, n, :], aw[n % 2][:, :], ALU.add).then_inc(x1_ready, 1)
                    else:
                        dve.wait_ge(x1_ready, n + 1)
                        norm_stats(2, n, x[:, n, :])
                elif step == "NC":
                    if piece == 0:
                        newton(2, n)
                    else:
                        if n < 2:
                            dve.wait_ge(v_psum, B)
                        else:
                            dve.wait_ge(xt2_psum, n - 1)
                        normalise(2, n, xn2[n % 2][:, :], x[:, n, :]).then_inc(xn2_ready, 1)
                elif step == "TY":
                    b, cols = n // TB, slice(n % TB * P, (n % TB + 1) * P)
                    dve.wait_ge(xt2_hi, n + 1)
                    if n == TB:
                        dve.wait_ge(wo_lo, KD)
                    dve.tensor_tensor(xl[b][:, :, cols], blocks(bank_of("TY", n)), xh[b][:, :, cols],
                                      ALU.subtract).then_inc(read_of("TY", n), 1)

            def clip_to_int8(p, m):
                y = ftmp[p % 2]["y"][0:m, :]
                dve.tensor_scalar(y, y, 127.0, -128.0, ALU.min, ALU.max).then_inc(clip_done, 1)

            def truncate(p, m, dst):
                f = ftmp[p % 2]
                rnd, above, absv = f["rnd"][0:m, :], f["above"][0:m, :], f["absv"][0:m, :]
                dve.wait_ge(abs_done, 2 * (p + 1))
                link(dve.tensor_scalar(rnd, absv, MAGIC, MAGIC, ALU.add, ALU.subtract))
                link(dve.tensor_tensor(above, rnd, absv, ALU.is_gt))
                link(dve.tensor_tensor(rnd, rnd, above, ALU.subtract))
                dve.tensor_tensor(dst, rnd, f["sign"][0:m, :], ALU.mult).then_inc(interq_ready, 1)

            def unit_out(p):
                it, b = UNITS[p] // 2, UNITS[p] % 2
                return interq[0:rows(it), it, b * S:(b + 1) * S]

            for p in range(2 * NF + 1):
                if p < 2 * NF:
                    m = rows(UNITS[p] // 2)
                    y = ftmp[p % 2]["y"][0:m, :]
                    dve.wait_ge(silu_done, p + 1)
                    dve.wait_ge(up_psum, p + 1)
                    dve.tensor_tensor(y, y, ps[0:m, FFB[p % 2][1], :], ALU.mult).then_inc(prod_done, 1)
                    dve.wait_ge(prod_done, p + 1)
                    clip_to_int8(p, m)
                if p >= 1:
                    truncate(p - 1, rows(UNITS[p - 1] // 2), unit_out(p - 1))

            for t in range(NT + 2):
                if t < NT:
                    dve.wait_ge(down_copied, t + 1)
                    clip_to_int8(2 * NF + t, P)
                if 1 <= t <= NT:
                    v = t - 1
                    p = 2 * NF + v
                    r = ftmp[p % 2]["rnd"][:, :]
                    if v >= 2:
                        dve.wait_ge(y_ready, v - 1)
                    truncate(p, P, r)
                    dve.wait_ge(interq_ready, p + 1)
                    norm_stats(3, v, r)
                if t >= 2:
                    v = t - 2
                    r = ftmp[v % 2]["rnd"][:, :]
                    dve.wait_ge(sd_ready[3], v + 1)
                    link(dve.reciprocal(rstd[:, 3, v:v + 1], sd[:, 3, v:v + 1]))
                    normalise(3, v, r, r).then_inc(y_normed, 1)
            dve.wait_ge(y_normed, NT)
            dve.tensor_tensor(x[:, NT - 1, :], x[:, NT - 1, :], ftmp[(NT - 1) % 2]["rnd"][:, :],
                              ALU.add).then_inc(last_ready, 1)

        @block.tensor
        def _(pe):
            def transpose_tile(k, src, signal):
                for i in range(KD):
                    ins = pe.transpose(ps[:, k, i * P:(i + 1) * P], src[:, i * P:(i + 1) * P], identf[:, :])
                ins.then_inc(signal, 1)

            def product_piece(k, piece, operands, signal):
                for j in range(piece * 3, piece * 3 + 3):
                    ins = pe.matmul(bank(k), *operands[j], start=(j == 0), stop=(j == 3 * KD - 1),
                                    skip_group_check=True)
                if piece == PIECES - 1:
                    ins.then_inc(signal, 1)

            def ffn_half(p, j, signal):
                u = UNITS[p]
                it, b = u // 2, u % 2
                m = rows(it)
                n = 0
                for w, xx in ((guh, xh), (guh, xl), (gul, xh)):
                    for k in range(KD):
                        ins = pe.matmul(ps[0:m, FFB[p % 2][j], :], w[it % 2][:, k, j, 0:m], xx[b][:, k, :],
                                        start=(n == 0), stop=(n == 3 * KD - 1))
                        n += 1
                ins.then_inc(signal, 1)

            for step, n, piece in steps:
                kind = kind_of(step)
                if step in BANKED and piece == 0:
                    wait_free(pe, step, n)
                if step == "TX":
                    pe.wait_ge(xn_ready, n + 1)
                    if n == 0:
                        pe.wait_ge(eye_loaded, 16)
                    transpose_tile(bank_of("TX", n), xn_of(n), xt_psum)
                elif step == "PJ":
                    b, m = n // NPROJ, n % NPROJ
                    if m == 0 and piece == 0:
                        for t in range(TB * b, TB * b + TB):
                            wait_read(pe, "TX", t)
                    if n == 0:
                        if piece < 2:
                            pe.wait_ge(wq_hi, min(3 * piece + 3, KD))
                        elif piece >= 2:
                            pe.wait_ge(wq_lo, 1 if piece == 2 else KD)
                    w = slice(m * P, (m + 1) * P)
                    operands = [(a[:, k, w], xx[b][:, k, :]) for a, xx in ((wqh, xh), (wqh, xl), (wql, xh))
                                for k in range(KD)]
                    product_piece(bank_of("PJ", n), piece, operands, proj_done)
                elif step == "VT":
                    wait_read(pe, "PJ", NPROJ * n + NQK)
                    transpose_tile(bank_of("VT", n), vT, v_psum)
                elif kind == "B":
                    b, g = n // NKV, n % NKV
                    if n == 0 and step == "B0":
                        pe.wait_ge(sel_ready, 14)
                    if step == "B2":
                        sh, sl, m = selkh[:, g, :, :, :], selkl[:, g, :, :, :], 0
                    else:
                        h = G * g + 2 * int(step[1])
                        m, r = 1 + h // 8, h % 8
                        sh, sl = selqh[:, r:r + 2, :, :], selql[:, r:r + 2, :, :]
                    sh, sl = (w.rearrange("p a s d -> p (a s d)") for w in (sh, sl))
                    pe.wait_ge(qk_lo, NQK * b + m + 1)
                    pe.matmul(bank(MI), sh, qkh[b][:, m, :], start=True, stop=False)
                    pe.matmul(bank(MI), sl, qkl[b][:, m, :], start=False, stop=True).then_inc(stack_psum, 1)
                elif kind == "M":
                    s = int(step[1:])
                    i, heads, nk = MAX_STEPS[s]
                    q, kk = qst[n % NB], kst[n % NB]
                    c = NM * n + s
                    if s == 0:
                        wait_read(pe, "B2", n)
                    if c == 0:
                        pe.wait_ge(consts_ready, 9)
                    if c < 2 and last_read(MXB[c], FIRST_USES) > 0:
                        pe.wait_ge(bank_read[MXB[c]], last_read(MXB[c], FIRST_USES))
                    if c >= 2:
                        pe.wait_ge(max_red, c - 1)
                    dst = bank(MXB[c % 2])
                    qs = slice(i * P, (i + 1) * P)
                    if i == 0:
                        for pr in range(NPAIR):
                            pe.matmul(dst[:, pr * 2 * P:(pr + 1) * 2 * P], q[:, pr, qs], kk[:, :, 0:nk],
                                      start=(pr == 0), stop=False, skip_group_check=True)
                    elif i == 1:
                        pe.matmul(dst, q[:, heads[0] // 2, qs], kk[:, :, 0:nk], start=True, stop=False,
                                  skip_group_check=True)
                    else:
                        h = heads[0]
                        pe.matmul(dst[:, 0:nk], q[:, h // 2, qs], kk[:, h % 2, 0:nk], start=True, stop=False,
                                  skip_group_check=True)
                    nh = len(heads)
                    diag = dst[:, 0:nh * nk].rearrange("p (h k) -> p h k", k=nk)[:, :, nk - P:nk]
                    pe.matmul(diag, identb[:, :], maskb[:, :].unsqueeze(1).broadcast_to([P, nh, P]),
                              start=False, stop=True, skip_group_check=True).then_inc(max_psum, 1)
                elif step == "MT":
                    pe.wait_ge(max_split, 2 * (n + 1))
                    for i in range(TB):
                        ins = pe.transpose(ps[0:2 * G, MI, i * P:(i + 1) * P],
                                           ms[n % 2][:, i, :, :].rearrange("p h a -> p (h a)").bitcast(F32),
                                           identf[:, :])
                    ins.then_inc(mt_psum, 1)
                elif kind == "S":
                    s = int(step[1:])
                    kb, pairs, halves = SCORE_STEPS[s]
                    q, kk = qst[n % NB], kst[n % NB]
                    c = NS * n + s
                    k = SC[c % 3]
                    if s == 0:
                        pe.wait_ge(mrow_sent[n % NB], 16 * G * (n // NB + 1))
                    if c < 3:
                        pe.wait_ge(bank_read[k], last_read(k, FIRST_USES))
                    if c >= 3:
                        pe.wait_ge(exp_done, c - 2)
                    nq = S - kb * P
                    w = len(pairs) * nq
                    for j, ab in enumerate(halves):
                        ins = pe.matmul(ps[:, k, j * w:(j + 1) * w].rearrange("p (a q) -> p a q", q=nq),
                                        kk[:, ab, kb * P:(kb + 1) * P],
                                        q[:, pairs[0]:pairs[-1] + 1, kb * P:S],
                                        start=True, stop=True, skip_group_check=True)
                    ins.then_inc(score_psum, 1)
                elif kind == "PV":
                    b, g, kb = n // NKV, n % NKV, int(step[2:])
                    nq = S - kb * P
                    if n % NKV == 0 and kb == 0:
                        wait_read(pe, "VT", b)
                    if n == 0 and kb == 0:
                        pe.wait_ge(bank_read[PVB], last_read(PVB, FIRST_USES))
                    pe.wait_ge(masked, TB * n + kb + 1)
                    if kb == 0 and n >= 1:
                        pe.wait_ge(ot_copied, n)
                    for h in range(G):
                        slot = h if kb < 2 else (h % 2) * NPAIR + h // 2
                        first = PROBS_AT[kb] + slot * nq
                        ins = pe.matmul(ps[32 * h:32 * h + HD + 1, PVB, kb * P:S],
                                        vone[:, TB * b + kb, g, 0:HD + 1], probs[:, first:first + nq],
                                        start=(kb == 0), stop=(kb == TB - 1), skip_group_check=True)
                    ins.then_inc(pv_done, 1)
                elif step == "OT":
                    pe.wait_ge(ot_copied, n + 1)
                    transpose_tile(MI, ots, ot_psum)
                elif step == "OR":
                    b, tb = n // TB, n % TB
                    if bank_of("OR", n) == 7 and tb == 0:
                        wait_read(pe, "OT", NKV * b + NKV - 1)
                    transpose_tile(bank_of("OR", n), o[b][:, tb, :], or_psum)
                elif step == "WO":
                    k = bank_of("WO", n)
                    if piece == 0:
                        wait_read(pe, "OR", n)
                        if n == 0:
                            pe.wait_ge(wo_lo, KD)
                        if n in (TB, TB + 1):
                            pe.wait_ge(max_red, NM * ITERS)
                    operands = [(a[ot_of(n)][:, i, :], w[:, i, :])
                                for a, w in ((oth, woh), (oth, wol), (otl, woh))
                                for i in range(KD)]
                    product_piece(k, piece, operands, wo_psum)
                elif step == "TY":
                    pe.wait_ge(xn2_ready, n + 1)
                    transpose_tile(bank_of("TY", n), xn2[n % 2], xt2_psum)
                elif step == "FG":
                    p = UNITS.index(n)
                    pe.wait_ge(gu_lo, KD * (n // 2 + 1))
                    wait_read(pe, "TY", TB - 1)
                    pe.wait_ge(exp_done, NS * ITERS)
                    pe.wait_ge(ot_copied, ITERS)
                    ffn_half(p, 0, gate_psum)
                elif step == "FU":
                    ffn_half(UNITS.index(n), 1, up_psum)

            for t in range(TB, NT):
                wait_read(pe, "TY", t)
            for p in range(2, 2 * NF):
                pe.wait_ge(gu_lo, KD * (UNITS[p] // 2 + 1))
                pe.wait_ge(prod_done, p - 1)
                ffn_half(p, 0, gate_psum)
                ffn_half(p, 1, up_psum)
            pe.wait_ge(wd_lo, NF)
            for t in range(NT):
                k = DNB[t % 4]
                pe.wait_ge(interq_ready, 2 * NF - (t < TB))
                if t < 4:
                    pe.wait_ge(bank_read[k], last_read(k, BANKED))
                else:
                    pe.wait_ge(down_copied, t - 3)
                for it in range(NF):
                    m = rows(it)
                    for w in (wdh, wdl):
                        ins = pe.matmul(bank(k), interq[0:m, it, t * P:(t + 1) * P], w[0:m, it, :],
                                        start=(it == 0 and w is wdh), stop=(it == NF - 1 and w is wdl))
                ins.then_inc(down_psum, 1)


def rope_tables():
    inv_freq = np.float32(1.0) / np.power(np.float32(10000.0), np.arange(0, HD, 2, dtype=np.float32) / HD)
    freqs = np.arange(S, dtype=np.float32)[:, None] * inv_freq[None, :].astype(np.float32)
    emb = np.concatenate([freqs, freqs], axis=-1)
    sign = np.where(np.arange(HD) < HD // 2, -1.0, 1.0)
    cos = np.cos(emb).astype(np.float32).T
    sin = (np.sin(emb) * sign[None, :]).astype(np.float32).T
    return np.tile(cos, (P // HD, 1)), np.tile(sin, (P // HD, 1))


def kernel(L0_attn_hidden_states, L0_attn_Wq, L0_attn_Wk, L0_attn_Wv, L0_attn_Wo, L0_ffn_w_gate,
           L0_ffn_w_up, L0_ffn_w_down):
    import concourse.bacc as bacc
    from concourse.bass_utils import run_bass_kernel_spmd

    cos, sin = rope_tables()
    arrays = {
        "x": np.asarray(L0_attn_hidden_states).reshape(TOK, D),
        "wqkvT": np.concatenate([np.asarray(w).T for w in (L0_attn_Wk, L0_attn_Wq, L0_attn_Wv)], axis=1),
        "woT": np.asarray(L0_attn_Wo).T,
        "wguT": np.stack([np.asarray(L0_ffn_w_gate).T, np.asarray(L0_ffn_w_up).T], axis=1),
        "wdT": np.asarray(L0_ffn_w_down).T,
        "cosT": cos,
        "sinT": sin,
        "eye": np.eye(P, dtype=np.float32),
    }
    arrays = {k: np.ascontiguousarray(a) for k, a in arrays.items()}
    nc = bacc.Bacc("TRN2", target_bir_lowering=False, num_devices=1)
    aps = [nc.dram_tensor(k, a.shape, mybir.dt.from_np(a.dtype), kind="ExternalInput").ap()
           for k, a in arrays.items()]
    out = nc.dram_tensor("out", (TOK, D), F32, kind="ExternalOutput").ap()
    layer_kernel(nc, *aps, out)
    r = run_bass_kernel_spmd(nc, [arrays], core_ids=[0])
    return r.results[0]["out"].reshape(B, S, D)
```

```python
from contextlib import ExitStack

import numpy as np

import concourse.bass as bass
from concourse import mybir

F32 = mybir.dt.float32
F32R = mybir.dt.float32r
BF16 = mybir.dt.bfloat16
ALU = mybir.AluOpType
ACT = mybir.ActivationFunctionType
AX = mybir.AxisListType

P = 128
B, S, D = 2, 512, 512
TOK = B * S
NT = TOK // P
TB = S // P
KD = D // P
NH, NKV, HD = 32, 8, 16
G = NH // NKV
NPAIR = G // 2
SLOT = 64
MROW = 3 * HD
QKVW = D + 2 * NKV * HD
NQK = (D + NKV * HD) // P
NPROJ = QKVW // P
F = 1376
NF = -(-F // P)
EPS = 1e-5
IN_SCALE = 128.0
OUT_SCALE = 128.0
NEG = -1.0e38
MAGIC = 8388608.0
SCALE = 1.0 / np.sqrt(HD)
ITERS = B * NKV
PIECES = 4

MAX_STEPS = [(0, (0, 1, 2, 3), P)] + [(1, (0, 1), 2 * P), (1, (2, 3), 2 * P)] \
    + [(i, (h,), (i + 1) * P) for i in (2, 3) for h in range(G)]
SCORE_STEPS = [(kb, (pr,), (ab,)) for kb in (0, 1) for pr in range(NPAIR) for ab in range(2)] \
    + [(2, (0, 1), (0,)), (2, (0, 1), (1,)), (3, (0, 1), (0, 1))]
NM, NS = len(MAX_STEPS), len(SCORE_STEPS)
SCORES_OF = [sum(kb <= b for kb, _, _ in SCORE_STEPS) for b in range(TB)]
PROBS_AT = [sum(G * (S - k * P) for k in range(kb)) for kb in range(TB + 1)]
BODY = ["M0", "S4", "M1", "MT", "S5", "PV0", "M2", "S6", "M3", "S7", "OT", "M4", "S8", "M5", "S9", "S10",
        "M6", "PV1", "B0", "M7", "PV2", "M8", "B1", "S0", "M9", "PV3", "S1", "B2", "M10", "S2", "MS", "S3", "OC"]
LAG = {"B": 0, "M": 1, "MS": 1, "MT": 2, "S": 3, "PV": 3, "OC": 3, "OT": 4}
EARLY = ("S0", "S1", "S2", "S3")
NR = 3
SEL_PARTS = 3 + 2 + 2 * 7
NB = 3


def kind_of(step):
    return step if step in ("MS", "MT", "OC", "OT") else step.rstrip("0123456789")


def iteration(step, j):
    return j - LAG[kind_of(step)] + (step in EARLY)


def interleave(main, fill):
    out, done = [], 0
    for i, step in enumerate(main):
        out.append(step)
        upto = len(fill) * (i + 1) // len(main)
        out += fill[done:upto]
        done = upto
    return out + fill[done:]


def projection(b):
    out = []
    first, last = NPROJ * b, NPROJ * b + NQK
    for c in range(first, first + NPROJ):
        out += [("PJ", c, i) for i in range(PIECES)]
        out += [("RO", c, 0), ("RO", c, 1)] if c < last else [("VC", b, 0)]
        if c > first:
            out.append(("QH", c - 1, 0))
    return out + [("VT", b, 0)]


FILLS = [16, 16, 10, 9, 9, 7, 7, 9, 4, 4, 4, 4, 8, 8, 8, 9, 10, 12, 99, 0]
STEP_PIECES = {"WO": PIECES, "FG": PIECES, "FU": PIECES}


def pieces(names):
    out = []
    for name in names:
        step, i = name[:2], int(name[2:])
        out += [(step, i, k) for k in range(STEP_PIECES.get(step, 1))]
    return out


AFTER_0 = pieces(["OR0", "WO0", "NA0", "OR1", "EA0", "WO1", "NB0", "XA0", "NA1", "NS0", "EB0", "OR2", "EA1", "NC0",
                  "WO2", "NB1", "XA1", "NA2", "NS1", "TY0", "EB1", "OR3", "EA2", "NC1", "WO3", "NB2", "XA2", "NA3",
                  "NS2", "TY1", "EB2", "EA3", "NC2", "NB3", "XA3", "TY2", "NS3", "EB3", "NC3", "TY3"])
AFTER_1 = pieces(["OR4", "OR5", "WO4", "NA4", "OR6", "EA4", "WO5", "NB4", "XA4", "NA5", "OR7", "NS4", "EA5", "WO6",
                  "EB4", "NB5", "XA5", "NC4", "NA6", "NS5", "TY4", "EA6", "WO7", "EB5", "NB6", "XA6", "NC5", "NA7",
                  "NS6", "TY5", "FU0", "EA7", "EB6", "NB7", "XA7", "NC6", "FG2", "NS7", "TY6", "EB7", "FU2", "NC7",
                  "TY7"])


def schedule():
    out = pieces(["ST0", "ST1", "LB0", "ST2", "LB1", "ST3", "LB2", "LB3", "TX0", "TX1", "WH0", "TX2", "WH1", "TX3",
                  "WH2", "WH3"])
    out += [("WL", k, 0) for k in range(KD)] + [("SE", 0, 0)]
    first = projection(0)
    begin = first.index(("QH", NQK - 2, 0)) + 1
    out += first[:begin]
    fill = pieces(["ST4", "ST5", "ST6", "ST7", "LB4", "LB5"]) + first[begin:] \
        + pieces(["TX4", "LB6", "TX5", "LB7", "TX6", "TX7"]) + projection(1)
    fill.insert(fill.index(("VC", 1, 0)), ("WR", 0, 0))
    split_wo = [("WS", 0, k) for k in range(KD)]
    post = [("GW", it, k) for it in range(2) for k in range(KD)]
    post = interleave(AFTER_0, post) + pieces(["FG0"])
    for j in range(ITERS + max(LAG.values())):
        main = [(step, iteration(step, j), 0) for step in BODY if 0 <= iteration(step, j) < ITERS]
        if j == NKV + LAG["OT"]:
            fill = fill + split_wo + post
        n = min(FILLS[min(j, len(FILLS) - 1)], len(fill))
        out += interleave(main, fill[:n])
        fill = fill[n:]
    out += fill
    out += AFTER_1
    return out


UNITS = [0, 2, 1, 3] + list(range(4, 2 * NF))



def last_use(it):
    return UNITS.index(2 * it + 1) + 1


def bank_of(step, i):
    if step == "TX":
        return 4 + i if i < TB else (i - 2) % 4
    if step == "PJ":
        return i % 4 if i < NPROJ + 2 else 7
    if step in ("OT", "MT", "B0", "B1", "B2"):
        return 6
    if step == "VT" or i < TB:
        return 7
    return {"OR": 6 + i % 2, "WO": i % 2, "TY": 6 + i % 2}[step]


BANKED = ("TX", "PJ", "VT", "OT", "MT", "B0", "B1", "B2", "OR", "WO", "TY")


def bank_counts(steps):
    before, after, done = {}, {}, [0] * 8
    for step, i, piece in steps:
        if step in BANKED and piece == 0:
            k = bank_of(step, i)
            before[step, i] = done[k]
            done[k] += 2 if step == "B2" else 1
            after[step, i] = done[k]
    return before, after


def layer_kernel(nc, x_in, wqkvT, woT, wguT, wdT, cosT, sinT, eye, out):
    with ExitStack() as ctx:
        at = [16512]

        def place(name, shape, dt, offset=None):
            size = 4 if dt in (F32, F32R) else 2
            nbytes = int(np.prod(shape[1:])) * size
            if offset is None:
                offset = at[0]
                at[0] += -(-nbytes // 32) * 32
            return nc.alloc_sbuf_tensor_at(name, shape, dt, offset=offset), offset + nbytes

        def sem(name):
            return ctx.enter_context(nc.semaphore(name))

        x, _ = place("x", [P, NT, D], F32)
        a_x = at[0]
        xh = [place(f"xh{b}", [P, KD, S], F32R)[0] for b in range(B)]
        xl = [place(f"xl{b}", [P, KD, S], F32R)[0] for b in range(B)]
        a_xl1 = at[0] - 4 * KD * S
        a_wo = at[0]
        woh, _ = place("woh", [P, KD, D], F32R)
        wol, _ = place("wol", [P, KD, D], F32R)
        a_o1 = at[0]
        o = [None] * B
        o[1], a_o0 = place("o1", [P, TB, D], F32)
        o[0], _ = place("o0", [P, TB, D], F32)
        a_g = at[0]
        qk = [None] * B
        qk[0], _ = place("qk0", [P, NQK, 2, S], F32R)
        a_r2 = at[0]
        qk[1], _ = place("qk1", [P, NQK, 2, S], F32R)
        vone, _ = place("vone", [P, NT, NKV, 32], F32)
        cos_sb, _ = place("cos_sb", [P, S], F32)
        sin_sb, _ = place("sin_sb", [P, S], F32)
        selq, _ = place("selq", [P, 8, 4, HD], F32R)
        selk, _ = place("selk", [P, NKV, 2, 4, HD], F32R)
        a_r = at[0]
        at[0] = a_r2 + 2 * 4 * NF * D
        a_r += 4 * S * 2
        assert a_r <= at[0]
        a_r1 = at[0]
        qst = [place(f"qst{i}", [P, NPAIR, S], F32R)[0] for i in range(NB)]
        kst = [place(f"kst{i}", [P, 2, S], F32R)[0] for i in range(NB)]
        a_probs = at[0]
        probs, _ = place("probs", [P, PROBS_AT[-1]], F32)
        a_e = at[0]
        ots, _ = place("ots", [P, S], F32)
        mt, _ = place("mt", [2 * G, S], F32R)
        a_tmp = at[0]
        rope_u = [place(f"rope_u{i}", [P, S], F32)[0] for i in range(2)]
        a_s = at[0]
        rope_s = [place(f"rope_s{i}", [P, S], F32)[0] for i in range(2)]
        rope_u.append(place("rope_u2", [P, S], F32, a_r - 8 * S)[0])
        rope_s.append(place("rope_s2", [P, S], F32, a_r - 4 * S)[0])
        rope_h = [place(f"rope_h{i}", [P, S], F32R, a)[0] for i, a in enumerate((a_s, a_s + 4 * S, a_r - 4 * S))]
        a_xn = at[0]
        xn = [place(f"xn{i}", [P, D], F32)[0] for i in range(2)]
        identf, _ = place("identf", [P, P], F32)
        identb, _ = place("identb", [P, P], BF16)
        maskb, _ = place("maskb", [P, P], BF16)
        zerob, _ = place("zerob", [P, P], BF16)
        ones_row, _ = place("ones_row", [P, 1], F32)
        epsc, _ = place("epsc", [P, 1], F32)
        mx = [place(f"mx{i}", [P, TB, G], F32)[0] for i in range(2)]
        ms = [place(f"ms{i}", [P, TB, G, 2], F32R)[0] for i in range(2)]
        rden = [place(f"rden{i}", [P, TB, G], F32)[0] for i in range(2)]
        stats, _ = place("stats", [P, NT, 6], F32)
        mv, _ = place("mv", [P, 4, NT, 2], F32)
        sd, _ = place("sd", [P, 4, NT], F32)
        rstd, _ = place("rstd", [P, 4, NT], F32)
        guess, _ = place("guess", [P, 4, NT], F32)
        newt, _ = place("newt", [P, 4, NT], F32)
        assert at[0] <= 229368, at[0]

        vT, e = place("vT", [P, S], F32, a_r)
        assert e <= a_r1
        wq_raw, e = place("wq_raw", [P, KD, QKVW], F32, a_probs)
        assert e <= a_e
        wqh, e = place("wqh", [P, KD, QKVW], F32R, a_wo)
        wql, e = place("wql", [P, KD, QKVW], F32R, e)
        assert e <= a_o0
        wo_raw, _ = place("wo_raw", [P, KD, D], F32, a_xl1)
        oth, otl = [None] * 2, [None] * 2
        oth[0], e = place("oth0", [P, KD, P], F32R, a_tmp)
        otl[0], e = place("otl0", [P, KD, P], F32R, e)
        aw = [None] * 2
        aw[0], e = place("aw0", [P, D], F32, e)
        aw[1], e = place("aw1", [P, D], F32, e)
        oth[1], e = place("oth1", [P, KD, P], F32R, a_e)
        otl[1], e = place("otl1", [P, KD, P], F32R, e)
        xn2 = xn

        def ot_of(t):
            return 0 if t < TB else t % 2

        def xn_of(t):
            return (xn + rope_s)[t] if t < TB else xn[t % 2]

        guh, gul = [None] * 2, [None] * 2
        e = a_g
        for i in range(2):
            guh[i], e = place(f"guh{i}", [P, KD, 2, P], F32R, e)
            gul[i], e = place(f"gul{i}", [P, KD, 2, P], F32R, e)
        gu_raw, e = place("gu_raw", [P, KD, 2, P], F32, e)
        assert e <= a_r2
        wdh, e = place("wdh", [P, NF, D], F32R, a_r2)
        wdl, e = place("wdl", [P, NF, D], F32R, e)
        assert e <= a_r1
        wd_raw = [place(f"wd_raw{i}", [P, D], F32, a_wo + 4 * D * i)[0] for i in range(2)]
        interq, e = place("interq", [P, NF, TOK], F32R, a_r1)
        assert e <= a_e
        z, _ = place("z", [P, NT, D], F32, a_x)
        ftmp = []
        for i, a in ((0, a_o0), (1, a_o1)):
            names = {}
            for j, (k, dt) in enumerate((("y", F32), ("absv", F32), ("sign", BF16), ("rnd", BF16))):
                names[k] = place(f"f{i}_{k}", [P, S], dt, a + 4 * S * j)[0]
            names["above"] = place(f"f{i}_above", [P, S], BF16, a_e + 4 * S * i)[0]
            ftmp.append(names)

        ps = ctx.enter_context(nc.psum_tensor("ps", [P, 8, 512], F32))
        SC, PVB, MXB, MI = (0, 1, 2), 3, (4, 5), 6
        FFB = [(4, 5)] + [(2, 3), (0, 1)] * NF
        DNB = (4, 5, 6, 7)

        x_loaded = [sem(f"x_loaded{t}") for t in range(NT)]
        wq_loaded = [sem(f"wq_loaded{k}") for k in range(KD)]
        eye_loaded, rope_loaded = sem("eye_loaded"), sem("rope_loaded")
        wo_loaded = sem("wo_loaded")
        gu_loaded = [sem(f"gu_loaded{k}") for k in range(KD)]
        wd_loaded = [sem(f"wd_loaded{i}") for i in range(2)]
        out_stored = sem("out_stored")
        bank_read = [sem(f"bank_read{i}") for i in range(8)]
        consts_ready = sem("consts_ready")
        kzero_ready = sem("kzero_ready")
        sel_ready = sem("sel_ready")
        wq_hi, wq_lo = sem("wq_hi"), sem("wq_lo")
        wo_hi, wo_lo = sem("wo_hi"), sem("wo_lo")
        gu_hi, gu_lo = sem("gu_hi"), sem("gu_lo")
        wd_hi, wd_lo = sem("wd_hi"), sem("wd_lo")
        dve_step = sem("dve_step")
        act_step = sem("act_step")
        var_ready = [sem(f"var_ready{i}") for i in range(4)]
        sd_ready = [sem(f"sd_ready{i}") for i in range(4)]
        xn_ready, xn2_ready = sem("xn_ready"), sem("xn2_ready")
        xt_psum, xt2_psum = sem("xt_psum"), sem("xt2_psum")
        xt_hi, xt2_hi = sem("xt_hi"), sem("xt2_hi")
        proj_done = sem("proj_done")
        shuf_done = sem("shuf_done")
        rope_cos = sem("rope_cos")
        rope_sum = sem("rope_sum")
        qk_hi, qk_lo = sem("qk_hi"), sem("qk_lo")
        qk_moved = [sem(f"qk_moved{i}") for i in range(NR)]
        v_psum = sem("v_psum")
        stack_psum = sem("stack_psum")
        max_psum = sem("max_psum")
        max_red = sem("max_red")
        max_split = sem("max_split")
        mt_psum = sem("mt_psum")
        mrow_sent = [sem(f"mrow_sent{i}") for i in range(NB)]
        score_psum = sem("score_psum")
        exp_done = sem("exp_done")
        masked = sem("masked")
        pv_done = sem("pv_done")
        ot_copied, ot_psum = sem("ot_copied"), sem("ot_psum")
        rden_ready = sem("rden_ready")
        or_psum, or_hi = sem("or_psum"), sem("or_hi")
        wo_psum = sem("wo_psum")
        aw_normed = sem("aw_normed")
        x1_ready = sem("x1_ready")
        gate_psum, up_psum = sem("gate_psum"), sem("up_psum")
        silu_done = sem("silu_done")
        prod_done = sem("prod_done")
        abs_done = sem("abs_done")
        interq_ready = sem("interq_ready")
        down_psum = sem("down_psum")
        y_normed = sem("y_normed")
        y_ready = sem("y_ready")
        last_ready = sem("last_ready")

        block = ctx.enter_context(nc.Block())
        steps = schedule()
        before, after = bank_counts(steps)

        def bank(i):
            return ps[:, i, :]

        def blocks(i):
            return bank(i).rearrange("p (k q) -> p k q", q=P)

        def wait_read(engine, step, i):
            engine.wait_ge(bank_read[bank_of(step, i)], after[step, i])

        def wait_free(engine, step, i):
            if before[step, i] > 0:
                engine.wait_ge(bank_read[bank_of(step, i)], before[step, i])

        def read_of(step, i):
            return bank_read[bank_of(step, i)]

        def wait_moved(engine, i):
            engine.wait_ge(qk_moved[i % NR], 16 * 4 * (i // NR + 1))

        def last_read(k, names):
            return max([v for (s, i), v in after.items() if s in names and bank_of(s, i) == k] + [0])

        FIRST_USES = ("TX", "PJ", "VT")

        def weight_steps():
            for p in range(2 * NF):
                yield from weights_after(p)

        def weights_after(p):
            out = [("gu", it) for it in range(2, NF) if last_use(it - 2) == p + 1]
            return out + ([("wd", p)] if p < NF else [])

        def rows(it):
            return min(P, F - it * P)

        @block.sync
        def _(sp):
            xt = x_in.rearrange("(t p) d -> t p d", p=P)
            wq = wqkvT.rearrange("(k p) f -> k p f", p=P)
            sp.dma_start(x[:, 0, :], xt[0]).then_inc(x_loaded[0], 16)
            sp.dma_start(identf[:, :], eye).then_inc(eye_loaded, 16)
            for t in range(1, TB):
                sp.dma_start(x[:, t, :], xt[t]).then_inc(x_loaded[t], 16)
            for k in range(KD):
                sp.dma_start(wq_raw[:, k, :], wq[k]).then_inc(wq_loaded[k], 16)
            sp.dma_start(cos_sb[:, :], cosT).then_inc(rope_loaded, 16)
            sp.dma_start(sin_sb[:, :], sinT).then_inc(rope_loaded, 16)
            for t in range(TB, NT):
                sp.dma_start(x[:, t, :], xt[t]).then_inc(x_loaded[t], 16)
            for step, n, piece in steps:
                if step == "WR":
                    sp.wait_ge(proj_done, B * NPROJ)
                    sp.dma_start(wo_raw[:, :, :], woT.rearrange("(k p) n -> p k n", p=P)).then_inc(wo_loaded, 16)
                elif step == "QH":
                    b, m, i = n // NPROJ, n % NPROJ, n - n // NPROJ
                    sp.wait_ge(qk_lo, i + 1)
                    for e in range(2):
                        here, there = slice(SLOT * e, SLOT * (e + 1)), slice(SLOT * (1 - e), SLOT * (2 - e))
                        sp.dma_start(qk[b][here, m, e, :].bitcast(F32),
                                     rope_h[i % NR][here, :].bitcast(F32)).then_inc(qk_moved[i % NR], 16)
                        sp.dma_start(qk[b][there, m, e, :].bitcast(F32),
                                     rope_u[i % NR][here, :]).then_inc(qk_moved[i % NR], 16)
                elif step == "MT":
                    wait_read(sp, "MT", n)
                    for h in range(G):
                        r = SLOT * (h % 2) + MROW
                        sp.dma_start(qst[n % NB][r:r + 2, h // 2, :].bitcast(F32),
                                     mt[2 * h:2 * h + 2, :].bitcast(F32)).then_inc(mrow_sent[n % NB], 16)
                elif step == "GW":
                    if n == 0 and piece == 0:
                        sp.wait_ge(stack_psum, 3 * NKV)
                    if n == 1:
                        sp.wait_ge(gu_lo, piece + 1)
                    m = rows(n)
                    sp.dma_start(gu_raw[:, piece, :, 0:m],
                                 wguT[piece * P:(piece + 1) * P, :, n * P:n * P + m]).then_inc(gu_loaded[piece], 16)
            for kind, it in weight_steps():
                m = rows(it)
                if kind == "gu":
                    sp.wait_ge(gu_lo, KD * it)
                    for k in range(KD):
                        sp.dma_start(gu_raw[:, k, :, 0:m],
                                     wguT[k * P:(k + 1) * P, :, it * P:it * P + m]).then_inc(gu_loaded[k], 16)
                else:
                    if it == 0:
                        sp.wait_ge(wo_psum, NT)
                    if it >= 2:
                        sp.wait_ge(wd_lo, it - 1)
                    sp.dma_start(wd_raw[it % 2][0:m, :], wdT[it * P:it * P + m, :]).then_inc(wd_loaded[it % 2], 16)
            ot = out.rearrange("(t p) d -> t p d", p=P)
            for t in range(NT):
                if t < NT - 1:
                    sp.wait_ge(y_ready, t + 1)
                else:
                    sp.wait_ge(last_ready, 1)
                sp.dma_start(ot[t], x[:, t, :]).then_inc(out_stored, 16)
            sp.wait_ge(out_stored, 16 * NT)

        @block.gpsimd
        def _(pool):
            pool.memset(epsc[:, :], EPS).then_inc(consts_ready, 1)
            pool.memset(zerob[:, :], 0.0).then_inc(consts_ready, 1)
            pool.memset(ones_row[:, :], 0.0).then_inc(consts_ready, 1)
            pool.wait_ge(consts_ready, 3)
            pool.affine_select(out=maskb[:, :], in_=zerob[:, :], compare_op=ALU.is_ge, fill=NEG,
                               base=0, pattern=[[-1, P]], channel_multiplier=1).then_inc(consts_ready, 1)
            pool.affine_select(out=identb[:, :], in_=zerob[:, :], compare_op=ALU.not_equal, fill=1.0,
                               base=0, pattern=[[-1, P]], channel_multiplier=1).then_inc(consts_ready, 1)
            for i, r in enumerate((MROW, MROW + 1, SLOT + MROW, SLOT + MROW + 1)):
                pool.wait_ge(consts_ready, 5 + i)
                pool.affine_select(out=ones_row[:, :], in_=ones_row[:, :], compare_op=ALU.not_equal, fill=1.0,
                                   base=-r, pattern=[[0, 1]], channel_multiplier=1).then_inc(consts_ready, 1)
            pool.memset(selq[:, :, :, :].bitcast(F32), 0.0).then_inc(sel_ready, 1)
            pool.memset(selk[:, :, :, :, :].bitcast(F32), 0.0).then_inc(sel_ready, 1)
            pool.memset(vone[:, :, :, HD:32], 1.0).then_inc(sel_ready, 1)
            for i in range(NB):
                pool.memset(kst[i][:, :, :].bitcast(F32), 0.0).then_inc(kzero_ready, 1)
            for step, n, piece in steps:
                kind = kind_of(step)
                if step == "RO" and piece == 1:
                    i = n - n // NPROJ
                    wait_read(pool, "PJ", n)
                    pool.tensor_tensor(rope_u[i % NR][:, :], rope_u[i % NR][:, :], rope_s[i % NR][:, :],
                                       ALU.add).then_inc(rope_sum, 1)
                elif step == "WS":
                    pool.wait_ge(wo_hi, piece + 1)
                    pool.tensor_tensor(wol[:, piece, :], wo_raw[:, piece, :], woh[:, piece, :],
                                       ALU.subtract).then_inc(wo_lo, 1)
                elif kind == "S":
                    kb = int(SCORE_STEPS[int(step[1:])][0])
                    if int(step[1:]) != SCORES_OF[kb] - 1:
                        continue
                    nq = S - kb * P
                    pool.wait_ge(exp_done, NS * n + SCORES_OF[kb])
                    d = probs[:, PROBS_AT[kb]:PROBS_AT[kb + 1]].rearrange("p (h q) -> p h q", q=nq)[:, :, 0:P]
                    pool.affine_select(out=d, in_=d, compare_op=ALU.is_ge, fill=0.0, base=0,
                                       pattern=[[0, G], [1, P]], channel_multiplier=-1).then_inc(masked, 1)
                elif step == "XA":
                    pool.wait_ge(aw_normed, n + 1)
                    pool.tensor_tensor(x[:, n, :], x[:, n, :], aw[n % 2][:, :], ALU.add).then_inc(x1_ready, 1)
                elif step == "GW":
                    m = rows(n)
                    pool.wait_ge(gu_hi, KD * n + piece + 1)
                    pool.tensor_tensor(gul[n][:, piece, :, 0:m], gu_raw[:, piece, :, 0:m],
                                       guh[n][:, piece, :, 0:m], ALU.subtract).then_inc(gu_lo, 1)
            for kind, it in weight_steps():
                m = rows(it)
                if kind == "gu":
                    pool.wait_ge(gu_hi, KD * (it + 1))
                    pool.tensor_tensor(gul[it % 2][:, :, :, 0:m], gu_raw[:, :, :, 0:m],
                                       guh[it % 2][:, :, :, 0:m], ALU.subtract).then_inc(gu_lo, KD)
                else:
                    pool.wait_ge(wd_hi, it + 1)
                    pool.tensor_tensor(wdl[0:m, it, :], wd_raw[it % 2][0:m, :], wdh[0:m, it, :],
                                       ALU.subtract).then_inc(wd_lo, 1)
            for t in range(NT - 1):
                pool.wait_ge(y_normed, t + 1)
                pool.tensor_tensor(x[:, t, :], x[:, t, :], z[:, t, :], ALU.add).then_inc(y_ready, 1)

        @block.scalar
        def _(act):
            linked = [0]

            def guess_rstd(norm, t):
                act.wait_ge(var_ready[norm], t + 1)
                act.activation(sd[:, norm, t:t + 1], mv[:, norm, t, 1:2], ACT.Ln,
                               bias=epsc[:, 0:1]).then_inc(act_step, 1)
                linked[0] += 1
                act.wait_ge(act_step, linked[0])
                act.activation(guess[:, norm, t:t + 1], sd[:, norm, t:t + 1], ACT.Exp,
                               scale=-0.5).then_inc(sd_ready[norm], 1)

            def root(norm, t):
                act.wait_ge(var_ready[norm], t + 1)
                act.activation(sd[:, norm, t:t + 1], mv[:, norm, t, 1:2], ACT.Sqrt,
                               bias=epsc[:, 0:1]).then_inc(sd_ready[norm], 1)

            act.wait_ge(consts_ready, 9)
            for step, n, piece in steps:
                kind = kind_of(step)
                if step == "ST":
                    root(0, n)
                    if n == NT - 1:
                        act.preload_act_table_set("natural_log_exp_and_others")
                elif step == "WH":
                    act.wait_ge(wq_loaded[n], 16)
                    act.activation(wqh[:, n, :], wq_raw[:, n, :], ACT.Copy).then_inc(wq_hi, 1)
                elif step == "TX":
                    b, tb = n // TB, n % TB
                    act.wait_ge(xt_psum, n + 1)
                    act.activation(xh[b][:, :, tb * P:(tb + 1) * P], blocks(bank_of("TX", n)),
                                   ACT.Copy).then_inc(xt_hi, 1)
                elif step == "QH":
                    i = n - n // NPROJ
                    act.wait_ge(rope_sum, i + 1)
                    act.activation(rope_h[i % NR][:, :], rope_u[i % NR][:, :], ACT.Copy).then_inc(qk_hi, 1)
                elif step == "VC":
                    act.wait_ge(proj_done, NPROJ * (n + 1))
                    if n >= 1:
                        act.wait_ge(v_psum, n)
                    last = NPROJ * n + NQK
                    act.activation(vT[:, :], bank(bank_of("PJ", last)), ACT.Copy).then_inc(read_of("PJ", last), 1)
                elif step == "WS":
                    if piece == 0:
                        act.wait_ge(wo_loaded, 16)
                    act.activation(woh[:, piece, :], wo_raw[:, piece, :], ACT.Copy).then_inc(wo_hi, 1)
                elif step in ("B0", "B1"):
                    pr = int(step[1])
                    act.wait_ge(stack_psum, 3 * n + pr + 1)
                    if n >= NB and pr == 0:
                        act.wait_ge(score_psum, NS * (n - NB + 1))
                    act.activation(qst[n % NB][:, pr, :], bank(MI), ACT.Copy).then_inc(bank_read[MI], 1)
                elif step == "B2":
                    act.wait_ge(stack_psum, 3 * n + 3)
                    if n < NB:
                        act.wait_ge(kzero_ready, n + 1)
                    act.activation(kst[n % NB][0:SLOT, 0, :], ps[0:SLOT, MI, :], ACT.Identity,
                                   bias=ones_row[0:SLOT, 0:1]).then_inc(bank_read[MI], 1)
                elif step == "MT":
                    act.wait_ge(mt_psum, n + 1)
                    if n >= 1:
                        act.wait_ge(mrow_sent[(n - 1) % NB], 16 * G * ((n - 1) // NB + 1))
                    act.activation(mt[:, :], ps[0:2 * G, MI, :], ACT.Copy).then_inc(bank_read[MI], 1)
                elif kind == "S":
                    s = int(step[1:])
                    kb, pairs, halves = SCORE_STEPS[s]
                    c, w = NS * n + s, len(pairs) * len(halves) * (S - kb * P)
                    first = PROBS_AT[kb] + sum(w for k, _, _ in SCORE_STEPS[:s] if k == kb)
                    act.wait_ge(score_psum, c + 1)
                    if n >= 1:
                        act.wait_ge(pv_done, TB * (n - 1) + kb + 1)
                    act.activation(probs[:, first:first + w], ps[:, SC[c % 3], 0:w], ACT.Exp,
                                   scale=float(SCALE)).then_inc(exp_done, 1)
                elif step == "OC":
                    act.wait_ge(pv_done, TB * (n + 1))
                    if n >= 1:
                        act.wait_ge(ot_psum, n)
                    act.activation(ots[:, :], bank(PVB), ACT.Copy).then_inc(ot_copied, 1)
                elif step == "OR":
                    if n == 0:
                        for i in range(B * NQK - NR, B * NQK):
                            wait_moved(act, i)
                    if n > TB:
                        act.wait_ge(wo_psum, n - 1)
                    elif n >= 1:
                        act.wait_ge(wo_psum, n)
                    act.wait_ge(or_psum, n + 1)
                    act.activation(oth[ot_of(n)][:, :, :], blocks(bank_of("OR", n)), ACT.Copy).then_inc(or_hi, 1)
                elif step == "NA":
                    act.wait_ge(wo_psum, n + 1)
                    if n >= 2:
                        act.wait_ge(x1_ready, n - 1)
                    act.activation(aw[n % 2][:, :], bank(bank_of("WO", n)), ACT.Copy).then_inc(read_of("WO", n), 1)
                elif step == "EA":
                    guess_rstd(1, n)
                elif step == "EB":
                    guess_rstd(2, n)
                elif step == "TY":
                    b, tb = n // TB, n % TB
                    act.wait_ge(xt2_psum, n + 1)
                    act.activation(xh[b][:, :, tb * P:(tb + 1) * P], blocks(bank_of("TY", n)),
                                   ACT.Copy).then_inc(xt2_hi, 1)
                elif step == "GW":
                    m = rows(n)
                    act.wait_ge(gu_loaded[piece], 16 * (n + 1))
                    act.activation(guh[n][:, piece, :, 0:m], gu_raw[:, piece, :, 0:m], ACT.Copy).then_inc(gu_hi, 1)

            def split_gu(it):
                m = rows(it)
                for k in range(KD):
                    act.wait_ge(gu_loaded[k], 16 * (it + 1))
                act.wait_ge(up_psum, last_use(it - 2))
                act.activation(guh[it % 2][:, :, :, 0:m], gu_raw[:, :, :, 0:m], ACT.Copy).then_inc(gu_hi, KD)

            def split_wd(it):
                m = rows(it)
                act.wait_ge(wd_loaded[it % 2], 16 * (it // 2 + 1))
                act.activation(wdh[0:m, it, :], wd_raw[it % 2][0:m, :], ACT.Copy).then_inc(wd_hi, 1)

            def abs_and_sign(p, m, src, scale):
                f = ftmp[p % 2]
                if p >= 2:
                    act.wait_ge(interq_ready, p - 1)
                act.activation(f["absv"][0:m, :], src, ACT.Abs, scale=scale).then_inc(abs_done, 1)
                act.activation(f["sign"][0:m, :], src, ACT.Sign, scale=scale).then_inc(abs_done, 1)

            for p, u in enumerate(UNITS):
                m = rows(u // 2)
                act.wait_ge(gate_psum, p + 1)
                if p >= 2:
                    act.wait_ge(abs_done, 2 * (p - 1))
                act.activation(ftmp[p % 2]["y"][0:m, :], ps[0:m, FFB[p][0], :], ACT.Silu,
                               scale=1.0 / IN_SCALE).then_inc(silu_done, 1)
                act.wait_ge(prod_done, p + 1)
                abs_and_sign(p, m, ftmp[p % 2]["y"][0:m, :], 1.0)
                for kind, it in weights_after(p):
                    if kind == "gu":
                        split_gu(it)
                    else:
                        split_wd(it)
            for t in range(NT + 1):
                if t < NT:
                    act.wait_ge(down_psum, t + 1)
                    abs_and_sign(2 * NF + t, P, bank(DNB[t % 4]), OUT_SCALE)
                if t >= 1:
                    root(3, t - 1)

        @block.vector
        def _(dve):
            count = [0]

            def link(ins):
                count[0] += 1
                ins.then_inc(dve_step, 1)
                dve.wait_ge(dve_step, count[0])

            def norm_stats(norm, t, src):
                link(dve.bn_stats(stats[:, t, :], src))
                dve.bn_aggr(mv[:, norm, t, :], stats[:, t, :]).then_inc(var_ready[norm], 1)

            def newton(norm, t):
                dve.wait_ge(sd_ready[norm], t + 1)
                v, r, a = mv[:, norm, t, 1:2], guess[:, norm, t:t + 1], newt[:, norm, t:t + 1]
                link(dve.scalar_tensor_tensor(out=a, in0=v, scalar=EPS, in1=r, op0=ALU.add, op1=ALU.mult))
                link(dve.scalar_tensor_tensor(out=a, in0=a, scalar=-0.5, in1=r, op0=ALU.mult, op1=ALU.mult))
                link(dve.scalar_tensor_tensor(out=rstd[:, norm, t:t + 1], in0=a, scalar=1.5, in1=r,
                                              op0=ALU.add, op1=ALU.mult))

            def normalise(norm, t, dst, src):
                return dve.tensor_scalar(dst, src, mv[:, norm, t, 0:1], rstd[:, norm, t:t + 1],
                                         ALU.subtract, ALU.mult)

            swap = [(p & 16) | ((p + HD // 2) & 15) for p in range(32)]

            for step, n, piece in steps:
                kind = kind_of(step)
                if step == "ST":
                    dve.wait_ge(x_loaded[n], 16)
                    norm_stats(0, n, x[:, n, :])
                elif step == "LB":
                    dve.wait_ge(sd_ready[0], n + 1)
                    link(dve.reciprocal(rstd[:, 0, n:n + 1], sd[:, 0, n:n + 1]))
                    if n >= TB:
                        dve.wait_ge(xt_psum, max(n - 1, TB))
                    normalise(0, n, xn_of(n)[:, :], x[:, n, :]).then_inc(xn_ready, 1)
                elif step == "TX":
                    b, cols = n // TB, slice(n % TB * P, (n % TB + 1) * P)
                    dve.wait_ge(xt_hi, n + 1)
                    dve.tensor_tensor(xl[b][:, :, cols], blocks(bank_of("TX", n)), xh[b][:, :, cols],
                                      ALU.subtract).then_inc(read_of("TX", n), 1)
                elif step == "WL":
                    dve.wait_ge(wq_hi, n + 1)
                    dve.tensor_tensor(wql[:, n, :], wq_raw[:, n, :], wqh[:, n, :],
                                      ALU.subtract).then_inc(wq_lo, 1)
                elif step == "SE":
                    dve.wait_ge(eye_loaded, 16)
                    dve.wait_ge(sel_ready, 3)
                    eye8 = identf[:, :].rearrange("p (g d) -> p g d", d=HD)
                    for slot in (0, 1):
                        dve.tensor_copy(selq[:, :, slot, :], eye8).then_inc(sel_ready, 1)
                    for e in range(2):
                        here, there = slice(4 * e, 4 * e + 4), slice(4 - 4 * e, 8 - 4 * e)
                        dve.tensor_copy(selq[:, here, 2, :], eye8[:, there, :]).then_inc(sel_ready, 1)
                        for ab in range(2):
                            dve.tensor_copy(selk[:, here, ab, 0, :], eye8[:, here, :]).then_inc(sel_ready, 1)
                            dve.tensor_copy(selk[:, here, ab, 2, :], eye8[:, here, :]).then_inc(sel_ready, 1)
                            dve.tensor_copy(selk[:, here, ab, 1, :], eye8[:, there, :]).then_inc(sel_ready, 1)
                elif step == "RO":
                    i = n - n // NPROJ
                    src = bank(bank_of("PJ", n))
                    if piece == 0:
                        dve.wait_ge(proj_done, n + 1)
                        if n == 0:
                            dve.wait_ge(rope_loaded, 32)
                        if i >= NR:
                            wait_moved(dve, i - NR)
                        dve.stream_shuffle(rope_s[i % NR][:, :], src, swap).then_inc(shuf_done, 1)
                        dve.tensor_tensor(rope_u[i % NR][:, :], src, cos_sb[:, :], ALU.mult).then_inc(rope_cos, 1)
                    else:
                        dve.wait_ge(shuf_done, i + 1)
                        dve.wait_ge(rope_cos, i + 1)
                        dve.tensor_tensor(rope_s[i % NR][:, :], rope_s[i % NR][:, :], sin_sb[:, :],
                                          ALU.mult).then_inc(read_of("PJ", n), 1)
                elif step == "QH":
                    i = n - n // NPROJ
                    dve.wait_ge(qk_hi, i + 1)
                    dve.tensor_tensor(rope_u[i % NR][:, :], rope_u[i % NR][:, :], rope_h[i % NR][:, :],
                                      ALU.subtract).then_inc(qk_lo, 1)
                elif step == "VT":
                    dve.wait_ge(v_psum, n + 1)
                    dve.tensor_copy(vone[:, TB * n:TB * n + TB, :, 0:HD],
                                    bank(bank_of("VT", n)).rearrange("p (t g d) -> p t g d", t=TB,
                                                                     d=HD)).then_inc(read_of("VT", n), 1)
                elif kind == "M":
                    s = int(step[1:])
                    i, heads, nk = MAX_STEPS[s]
                    dve.wait_ge(max_psum, NM * n + s + 1)
                    if s == 0 and n >= 2:
                        dve.wait_ge(max_split, 2 * (n - 1))
                    src = bank(MXB[(NM * n + s) % 2])[:, 0:len(heads) * nk]
                    dve.tensor_reduce(mx[n % 2][:, i, heads[0]:heads[-1] + 1],
                                      src.rearrange("p (h k) -> p h k", k=nk), AX.X, ALU.max,
                                      negate=True).then_inc(max_red, 1)
                elif step == "MS":
                    dve.wait_ge(max_red, NM * (n + 1))
                    if n >= 2:
                        dve.wait_ge(mt_psum, n - 1)
                    dve.tensor_copy(ms[n % 2][:, :, :, 0], mx[n % 2][:, :, :]).then_inc(max_split, 1)
                    dve.wait_ge(max_split, 2 * n + 1)
                    dve.tensor_tensor(ms[n % 2][:, :, :, 1], mx[n % 2][:, :, :], ms[n % 2][:, :, :, 0],
                                      ALU.subtract).then_inc(max_split, 1)
                elif step == "B2":
                    dve.wait_ge(stack_psum, 3 * n + 3)
                    if n == 0:
                        dve.wait_ge(consts_ready, 9)
                    if n < NB:
                        dve.wait_ge(kzero_ready, n + 1)
                    else:
                        dve.wait_ge(score_psum, NS * (n - NB + 1))
                    dve.tensor_scalar(kst[n % NB][SLOT:P, 1, :], ps[SLOT:P, MI, :], ones_row[SLOT:P, 0:1], None,
                                      ALU.add).then_inc(bank_read[MI], 1)
                elif step == "OT":
                    b, g = n // NKV, n % NKV
                    dve.wait_ge(ot_psum, n + 1)
                    if n == NKV:
                        dve.wait_ge(proj_done, B * NPROJ)
                    o4 = bank(MI).rearrange("p (i h d) -> p i h d", i=TB, d=32)
                    dve.reciprocal(rden[n % 2][:, :, :], o4[:, :, :, HD]).then_inc(rden_ready, 1)
                    dve.wait_ge(rden_ready, n + 1)
                    dst = o[b][:, :, g * G * HD:(g + 1) * G * HD]
                    dve.tensor_tensor(dst.rearrange("p i (h d) -> p i h d", d=HD), o4[:, :, :, 0:HD],
                                      rden[n % 2][:, :, :].unsqueeze(3).broadcast_to([P, TB, G, HD]),
                                      ALU.mult).then_inc(bank_read[MI], 1)
                elif step == "OR":
                    dve.wait_ge(or_hi, n + 1)
                    dve.tensor_tensor(otl[ot_of(n)][:, :, :], blocks(bank_of("OR", n)), oth[ot_of(n)][:, :, :],
                                      ALU.subtract).then_inc(read_of("OR", n), 1)
                elif step == "NA":
                    wait_read(dve, "WO", n)
                    norm_stats(1, n, aw[n % 2][:, :])
                elif step == "NB":
                    newton(1, n)
                    normalise(1, n, aw[n % 2][:, :], aw[n % 2][:, :]).then_inc(aw_normed, 1)
                elif step == "NS":
                    dve.wait_ge(x1_ready, n + 1)
                    norm_stats(2, n, x[:, n, :])
                elif step == "NC":
                    newton(2, n)
                    if n < 2:
                        dve.wait_ge(xt_psum, NT)
                    else:
                        dve.wait_ge(xt2_psum, n - 1)
                    normalise(2, n, xn2[n % 2][:, :], x[:, n, :]).then_inc(xn2_ready, 1)
                elif step == "TY":
                    b, cols = n // TB, slice(n % TB * P, (n % TB + 1) * P)
                    dve.wait_ge(xt2_hi, n + 1)
                    if n == TB:
                        dve.wait_ge(wo_lo, KD)
                    dve.tensor_tensor(xl[b][:, :, cols], blocks(bank_of("TY", n)), xh[b][:, :, cols],
                                      ALU.subtract).then_inc(read_of("TY", n), 1)

            def truncate(p, m, dst):
                f = ftmp[p % 2]
                rnd, above, absv = f["rnd"][0:m, :], f["above"][0:m, :], f["absv"][0:m, :]
                dve.wait_ge(abs_done, 2 * (p + 1))
                link(dve.tensor_scalar(rnd, absv, MAGIC, MAGIC, ALU.add, ALU.subtract))
                link(dve.tensor_tensor(above, rnd, absv, ALU.is_gt))
                link(dve.tensor_tensor(rnd, rnd, above, ALU.subtract))
                link(dve.scalar_tensor_tensor(out=rnd, in0=rnd, scalar=128.0, in1=f["sign"][0:m, :],
                                              op0=ALU.min, op1=ALU.mult))
                dve.tensor_scalar(dst, rnd, 127.0, None, ALU.min).then_inc(interq_ready, 1)

            def unit_out(p):
                it, b = UNITS[p] // 2, UNITS[p] % 2
                return interq[0:rows(it), it, b * S:(b + 1) * S]

            for p in range(2 * NF + 1):
                if p == 2 * NF - 1:
                    truncate(p - 1, rows(UNITS[p - 1] // 2), unit_out(p - 1))
                if p < 2 * NF:
                    m = rows(UNITS[p] // 2)
                    y = ftmp[p % 2]["y"][0:m, :]
                    dve.wait_ge(silu_done, p + 1)
                    dve.wait_ge(up_psum, p + 1)
                    dve.tensor_tensor(y, y, ps[0:m, FFB[p][1], :], ALU.mult).then_inc(prod_done, 1)
                if p >= 1 and p != 2 * NF - 1:
                    truncate(p - 1, rows(UNITS[p - 1] // 2), unit_out(p - 1))

            for t in range(NT + 1):
                if t < NT:
                    truncate(2 * NF + t, P, z[:, t, :])
                    dve.wait_ge(interq_ready, 2 * NF + t + 1)
                    norm_stats(3, t, z[:, t, :])
                if t >= 1:
                    v = t - 1
                    dve.wait_ge(sd_ready[3], v + 1)
                    link(dve.reciprocal(rstd[:, 3, v:v + 1], sd[:, 3, v:v + 1]))
                    normalise(3, v, z[:, v, :], z[:, v, :]).then_inc(y_normed, 1)
            dve.wait_ge(y_normed, NT)
            dve.tensor_tensor(x[:, NT - 1, :], x[:, NT - 1, :], z[:, NT - 1, :], ALU.add).then_inc(last_ready, 1)

        @block.tensor
        def _(pe):
            def transpose_tile(k, src, signal):
                for i in range(KD):
                    ins = pe.transpose(ps[:, k, i * P:(i + 1) * P], src[:, i * P:(i + 1) * P], identf[:, :])
                ins.then_inc(signal, 1)

            def product_piece(k, piece, operands, signal):
                for j in range(piece * 3, piece * 3 + 3):
                    ins = pe.matmul(bank(k), *operands[j], start=(j == 0), stop=(j == 3 * KD - 1),
                                    skip_group_check=True)
                if piece == PIECES - 1:
                    ins.then_inc(signal, 1)

            def ffn_half(p, j, signal, pieces=range(PIECES)):
                u = UNITS[p]
                it, b = u // 2, u % 2
                m = rows(it)
                operands = [(w[it % 2][:, k, j, 0:m], xx[b][:, k, :])
                            for w, xx in ((guh, xh), (guh, xl), (gul, xh)) for k in range(KD)]
                for n in (3 * piece + i for piece in pieces for i in range(3)):
                    ins = pe.matmul(ps[0:m, FFB[p][j], :], *operands[n], start=(n == 0), stop=(n == 3 * KD - 1),
                                    skip_group_check=True)
                if PIECES - 1 in pieces:
                    ins.then_inc(signal, 1)

            for step, n, piece in steps:
                kind = kind_of(step)
                if step in BANKED and piece == 0:
                    wait_free(pe, step, n)
                if step == "TX":
                    pe.wait_ge(xn_ready, n + 1)
                    if n == 0:
                        pe.wait_ge(eye_loaded, 16)
                    transpose_tile(bank_of("TX", n), xn_of(n), xt_psum)
                elif step == "PJ":
                    b, m = n // NPROJ, n % NPROJ
                    if m == 0 and piece == 0:
                        for t in range(TB * b, TB * b + TB):
                            wait_read(pe, "TX", t)
                    if n == 0:
                        if piece < 2:
                            pe.wait_ge(wq_hi, min(3 * piece + 3, KD))
                        elif piece >= 2:
                            pe.wait_ge(wq_lo, 1 if piece == 2 else KD)
                    w = slice(m * P, (m + 1) * P)
                    operands = [(a[:, k, w], xx[b][:, k, :]) for a, xx in ((wqh, xh), (wqh, xl), (wql, xh))
                                for k in range(KD)]
                    product_piece(bank_of("PJ", n), piece, operands, proj_done)
                elif step == "VT":
                    wait_read(pe, "PJ", NPROJ * n + NQK)
                    transpose_tile(bank_of("VT", n), vT, v_psum)
                elif kind == "B":
                    b, g = n // NKV, n % NKV
                    if n == 0 and step == "B0":
                        pe.wait_ge(sel_ready, SEL_PARTS)
                    if step == "B2":
                        m, e, select = 0, g // 4, selk[:, g, :, :, :]
                    else:
                        h = G * g + 2 * int(step[1])
                        m, e, select = 1 + h // 8, h % 8 // 4, selq[:, h % 8:h % 8 + 2, :, :]
                    wait_moved(pe, NQK * b + m)
                    pe.matmul(bank(MI), select.rearrange("p a s d -> p (a s d)"), qk[b][:, m, e, :],
                              start=True, stop=True).then_inc(stack_psum, 1)
                elif kind == "M":
                    s = int(step[1:])
                    i, heads, nk = MAX_STEPS[s]
                    q, kk = qst[n % NB], kst[n % NB]
                    c = NM * n + s
                    if s == 0:
                        wait_read(pe, "B2", n)
                    if c == 0:
                        pe.wait_ge(consts_ready, 9)
                    if c < 2 and last_read(MXB[c], FIRST_USES) > 0:
                        pe.wait_ge(bank_read[MXB[c]], last_read(MXB[c], FIRST_USES))
                    if c >= 2:
                        pe.wait_ge(max_red, c - 1)
                    dst = bank(MXB[c % 2])
                    qs = slice(i * P, (i + 1) * P)
                    if i == 0:
                        for pr in range(NPAIR):
                            pe.matmul(dst[:, pr * 2 * P:(pr + 1) * 2 * P], q[:, pr, qs], kk[:, :, 0:nk],
                                      start=(pr == 0), stop=False, skip_group_check=True)
                    elif i == 1:
                        pe.matmul(dst, q[:, heads[0] // 2, qs], kk[:, :, 0:nk], start=True, stop=False,
                                  skip_group_check=True)
                    else:
                        h = heads[0]
                        pe.matmul(dst[:, 0:nk], q[:, h // 2, qs], kk[:, h % 2, 0:nk], start=True, stop=False,
                                  skip_group_check=True)
                    nh = len(heads)
                    diag = dst[:, 0:nh * nk].rearrange("p (h k) -> p h k", k=nk)[:, :, nk - P:nk]
                    pe.matmul(diag, identb[:, :], maskb[:, :].unsqueeze(1).broadcast_to([P, nh, P]),
                              start=False, stop=True, skip_group_check=True).then_inc(max_psum, 1)
                elif step == "MT":
                    pe.wait_ge(max_split, 2 * (n + 1))
                    for i in range(TB):
                        ins = pe.transpose(ps[0:2 * G, MI, i * P:(i + 1) * P],
                                           ms[n % 2][:, i, :, :].rearrange("p h a -> p (h a)").bitcast(F32),
                                           identf[:, :])
                    ins.then_inc(mt_psum, 1)
                elif kind == "S":
                    s = int(step[1:])
                    kb, pairs, halves = SCORE_STEPS[s]
                    q, kk = qst[n % NB], kst[n % NB]
                    c = NS * n + s
                    k = SC[c % 3]
                    if s == 0:
                        pe.wait_ge(mrow_sent[n % NB], 16 * G * (n // NB + 1))
                    if c < 3:
                        pe.wait_ge(bank_read[k], last_read(k, FIRST_USES))
                    if c >= 3:
                        pe.wait_ge(exp_done, c - 2)
                    nq = S - kb * P
                    w = len(pairs) * nq
                    for j, ab in enumerate(halves):
                        ins = pe.matmul(ps[:, k, j * w:(j + 1) * w].rearrange("p (a q) -> p a q", q=nq),
                                        kk[:, ab, kb * P:(kb + 1) * P],
                                        q[:, pairs[0]:pairs[-1] + 1, kb * P:S],
                                        start=True, stop=True, skip_group_check=True)
                    ins.then_inc(score_psum, 1)
                elif kind == "PV":
                    b, g, kb = n // NKV, n % NKV, int(step[2:])
                    nq = S - kb * P
                    if n % NKV == 0 and kb == 0:
                        wait_read(pe, "VT", b)
                    if n == 0 and kb == 0:
                        pe.wait_ge(bank_read[PVB], last_read(PVB, FIRST_USES))
                    pe.wait_ge(masked, TB * n + kb + 1)
                    if kb == 0 and n >= 1:
                        pe.wait_ge(ot_copied, n)
                    for h in range(G):
                        slot = h if kb < 2 else (h % 2) * NPAIR + h // 2
                        first = PROBS_AT[kb] + slot * nq
                        ins = pe.matmul(ps[32 * h:32 * h + HD + 1, PVB, kb * P:S],
                                        vone[:, TB * b + kb, g, 0:HD + 1], probs[:, first:first + nq],
                                        start=(kb == 0), stop=(kb == TB - 1), skip_group_check=True)
                    ins.then_inc(pv_done, 1)
                elif step == "OT":
                    pe.wait_ge(ot_copied, n + 1)
                    transpose_tile(MI, ots, ot_psum)
                elif step == "OR":
                    b, tb = n // TB, n % TB
                    if bank_of("OR", n) == 7 and tb == 0:
                        wait_read(pe, "OT", NKV * b + NKV - 1)
                    transpose_tile(bank_of("OR", n), o[b][:, tb, :], or_psum)
                elif step == "WO":
                    k = bank_of("WO", n)
                    if piece == 0:
                        wait_read(pe, "OR", n)
                        if n == 0:
                            pe.wait_ge(wo_lo, KD)
                        if n in (TB, TB + 1):
                            pe.wait_ge(exp_done, NS * ITERS)
                    operands = [(a[ot_of(n)][:, i, :], w[:, i, :])
                                for a, w in ((oth, woh), (oth, wol), (otl, woh))
                                for i in range(KD)]
                    product_piece(k, piece, operands, wo_psum)
                elif step == "TY":
                    pe.wait_ge(xn2_ready, n + 1)
                    transpose_tile(bank_of("TY", n), xn2[n % 2], xt2_psum)
                elif step == "FG":
                    p = UNITS.index(n)
                    pe.wait_ge(gu_lo, KD * (n // 2 + 1))
                    wait_read(pe, "TY", TB - 1)
                    if n == 0:
                        pe.wait_ge(max_red, NM * ITERS)
                    else:
                        pe.wait_ge(exp_done, NS * ITERS)
                        pe.wait_ge(ot_copied, ITERS)
                    ffn_half(p, 0, gate_psum, [piece])
                elif step == "FU":
                    ffn_half(UNITS.index(n), 1, up_psum, [piece])

            for t in range(TB, NT):
                wait_read(pe, "TY", t)
            for p in range(2, 2 * NF):
                pe.wait_ge(gu_lo, KD * (UNITS[p] // 2 + 1))
                if p == 2:
                    for t in (NT - 2, NT - 1):
                        wait_read(pe, "WO", t)
                else:
                    pe.wait_ge(prod_done, p - 1)
                ffn_half(p, 0, gate_psum)
                ffn_half(p, 1, up_psum)
            pe.wait_ge(wd_lo, NF)
            for t in range(NT):
                k = DNB[t % 4]
                pe.wait_ge(interq_ready, 2 * NF - (t < TB))
                if t < 4:
                    pe.wait_ge(bank_read[k], last_read(k, BANKED))
                    pe.wait_ge(prod_done, 1)
                else:
                    pe.wait_ge(abs_done, 2 * (2 * NF + t - 3))
                for it in range(NF):
                    m = rows(it)
                    for w in (wdh, wdl):
                        ins = pe.matmul(bank(k), interq[0:m, it, t * P:(t + 1) * P], w[0:m, it, :],
                                        start=(it == 0 and w is wdh), stop=(it == NF - 1 and w is wdl))
                ins.then_inc(down_psum, 1)


def rope_tables():
    inv_freq = np.float32(1.0) / np.power(np.float32(10000.0), np.arange(0, HD, 2, dtype=np.float32) / HD)
    freqs = np.arange(S, dtype=np.float32)[:, None] * inv_freq[None, :].astype(np.float32)
    emb = np.concatenate([freqs, freqs], axis=-1)
    sign = np.where(np.arange(HD) < HD // 2, -1.0, 1.0)
    cos = np.cos(emb).astype(np.float32).T
    sin = (np.sin(emb) * sign[None, :]).astype(np.float32).T
    return np.tile(cos, (P // HD, 1)), np.tile(sin, (P // HD, 1))


def kernel(L0_attn_hidden_states, L0_attn_Wq, L0_attn_Wk, L0_attn_Wv, L0_attn_Wo, L0_ffn_w_gate,
           L0_ffn_w_up, L0_ffn_w_down):
    import concourse.bacc as bacc
    from concourse.bass_utils import run_bass_kernel_spmd

    cos, sin = rope_tables()
    arrays = {
        "x": np.asarray(L0_attn_hidden_states).reshape(TOK, D),
        "wqkvT": np.concatenate([np.asarray(w).T for w in (L0_attn_Wk, L0_attn_Wq, L0_attn_Wv)], axis=1),
        "woT": np.asarray(L0_attn_Wo).T,
        "wguT": np.stack([np.asarray(L0_ffn_w_gate).T, np.asarray(L0_ffn_w_up).T], axis=1),
        "wdT": np.asarray(L0_ffn_w_down).T,
        "cosT": cos,
        "sinT": sin,
        "eye": np.eye(P, dtype=np.float32),
    }
    arrays = {k: np.ascontiguousarray(a) for k, a in arrays.items()}
    nc = bacc.Bacc("TRN2", target_bir_lowering=False, num_devices=1)
    aps = [nc.dram_tensor(k, a.shape, mybir.dt.from_np(a.dtype), kind="ExternalInput").ap()
           for k, a in arrays.items()]
    out = nc.dram_tensor("out", (TOK, D), F32, kind="ExternalOutput").ap()
    layer_kernel(nc, *aps, out)
    r = run_bass_kernel_spmd(nc, [arrays], core_ids=[0])
    return r.results[0]["out"].reshape(B, S, D)
```
